# Optimizing a Trainium2 kernel written in Bass

```python
import numpy as np
import jax
import jax.numpy as jnp

def _softmax(x, axis=-1):
    return jax.nn.softmax(x, axis=axis)

def _gelu(x):
    return jax.nn.gelu(x, approximate=True)

def _silu(x):
    return jax.nn.silu(x)

def _sigmoid(x):
    return jax.nn.sigmoid(x)

def _layernorm(x, axis=-1, eps=1e-05):
    m = jnp.mean(x, axis=axis, keepdims=True)
    v = jnp.var(x, axis=axis, keepdims=True)
    return (x - m) / jnp.sqrt(v + eps)

def _scatter_add(tgt, idx, src, axis=0):
    return tgt.at[idx].add(src)

def _segment_sum(src, seg, n):
    return jax.ops.segment_sum(src, seg, n)
kernel_name = 'mk_perceiver_d1_seqx_r4_549bbc'

def setup_inputs(seed: int=0):
    np.random.seed(seed)
    _w = jnp.asarray

    def _rec_inputs():
        import jax
        import jax.numpy as jnp
        _rk = jax.random.key(seed)
        x = 7.22e-05 + 1 * jax.random.normal(jax.random.fold_in(_rk, 1), (64, 32, 256), jnp.float32)
        _lenS = 32 - jax.random.randint(jax.random.fold_in(_rk, 7), (64,), 0, max(1, 32 // 4) + 1, jnp.int32)
        _lenS2 = 257 - jax.random.randint(jax.random.fold_in(_rk, 8), (64,), 0, max(1, 257 // 4) + 1, jnp.int32)
        _ctx_768P = jax.random.normal(jax.random.fold_in(_rk, 11), (64, 16, 192), jnp.float32)
        _ctx_768c = jax.random.dirichlet(jax.random.fold_in(_rk, 511), 0.3 * jnp.ones((16,), jnp.float32), (64, 257))
        _ctx_768t = jnp.einsum('bsk,bkd->bsd', _ctx_768c, _ctx_768P)
        _ctx_768t = _ctx_768t * jax.lax.rsqrt(jnp.mean(jnp.square(_ctx_768t)) + 1e-12) * 0.953939
        ctx_768 = -0.000191848 + 0.999787 * (_ctx_768t + 0.3 * jax.random.normal(jax.random.fold_in(_rk, 611), (64, 257, 192), jnp.float32))
        return (x, ctx_768)
    x, ctx_768 = _rec_inputs()

    def _L0_xattn_setup():
        import jax, jax.numpy as jnp
        import numpy as np
        NUM_HEADS = 16
        CLAMP = 10000.0
        key = jax.random.key(seed)
        ks = jax.random.split(key, 8)
        B, Nq, Nkv, Cq, Ckv = (4, 512, 512, 256, 192)
        s_q = 1.0 / np.sqrt(Cq)
        s_kv = 1.0 / np.sqrt(Ckv)
        return {'query': jax.random.normal(ks[0], (B, Nq, Cq), jnp.float32), 'key_value': jax.random.normal(ks[1], (B, Nkv, Ckv), jnp.float32), 'Wq': jax.random.normal(ks[2], (Cq, Cq), jnp.float32) * s_q, 'bq': jnp.zeros((Cq,), jnp.float32), 'Wk': jax.random.normal(ks[3], (Ckv, Cq), jnp.float32) * s_kv, 'bk': jnp.zeros((Cq,), jnp.float32), 'Wv': jax.random.normal(ks[4], (Ckv, Cq), jnp.float32) * s_kv, 'bv': jnp.zeros((Cq,), jnp.float32), 'Wo': jax.random.normal(ks[5], (Cq, Cq), jnp.float32) * s_q, 'bo': jnp.zeros((Cq,), jnp.float32)}
    _L0_xattn_all = _L0_xattn_setup()
    _L0_xattn_in = {k: v for k, v in _L0_xattn_all.items() if k in ('Wq', 'bq', 'Wk', 'bk', 'Wv', 'bv', 'Wo', 'bo')}
    del _L0_xattn_all

    def _L0_attn_setup():
        import jax, jax.numpy as jnp
        import numpy as np
        D_MODEL = 256
        NUM_HEADS = 16
        HEAD_DIM = D_MODEL // NUM_HEADS
        ALPHA = 1.0
        key = jax.random.key(seed)
        ks = jax.random.split(key, 9)
        B, T, D = (2, 512, D_MODEL)
        s = 1.0 / np.sqrt(D)
        inp = {'x': jax.random.normal(ks[0], (B, T, D), dtype=jnp.float32), 'Wq': jax.random.uniform(ks[1], (D, D), jnp.float32, -s, s), 'bq': jax.random.uniform(ks[2], (D,), jnp.float32, -s, s), 'Wk': jax.random.uniform(ks[3], (D, D), jnp.float32, -s, s), 'bk': jax.random.uniform(ks[4], (D,), jnp.float32, -s, s), 'Wv': jax.random.uniform(ks[5], (D, D), jnp.float32, -s, s), 'bv': jax.random.uniform(ks[6], (D,), jnp.float32, -s, s), 'Wo': jax.random.uniform(ks[7], (D, D), jnp.float32, -s, s), 'bo': jax.random.uniform(ks[8], (D,), jnp.float32, -s, s)}
        return inp
    _L0_attn_all = _L0_attn_setup()
    _L0_attn_in = {k: v for k, v in _L0_attn_all.items() if k in ('Wq', 'bq', 'Wk', 'bk', 'Wv', 'bv', 'Wo', 'bo')}
    del _L0_attn_all

    def _L0_ffn_setup():
        import jax, jax.numpy as jnp
        import numpy as np
        B, T, C, H, E, K = (4, 256, 256, 256, 8, 2)

        def _swiglu(x):
            a, b = jnp.split(x, 2, axis=-1)
            return jax.nn.silu(a) * b
        key = jax.random.key(seed)
        ks = jax.random.split(key, 6)
        s = 0.02
        x = jax.random.normal(ks[0], (B, T, C), jnp.float32)
        w_shared_in = jax.random.normal(ks[1], (C, 2 * H), jnp.float32) * s
        w_shared_out = jax.random.normal(ks[2], (H, C), jnp.float32) * s
        w1_shared = jax.random.normal(ks[3], (C, 2 * H), jnp.float32) * s
        w2 = jax.random.normal(ks[4], (E, H, C), jnp.float32) * s
        w_gate = jax.random.normal(ks[5], (C, E), jnp.float32) * s
        gate_bias = jnp.zeros((E,), jnp.float32)
        return {'x': x, 'w_shared_in': w_shared_in, 'w_shared_out': w_shared_out, 'w1_shared': w1_shared, 'w2': w2, 'w_gate': w_gate, 'gate_bias': gate_bias}
    _L0_ffn_all = _L0_ffn_setup()
    _L0_ffn_in = {k: v for k, v in _L0_ffn_all.items() if k in ('w_shared_in', 'w_shared_out', 'w1_shared', 'w2', 'w_gate', 'gate_bias')}
    del _L0_ffn_all
    return {'x': x, 'ctx_768': ctx_768, 'L0_xattn_Wq': _L0_xattn_in['Wq'], 'L0_xattn_bq': _L0_xattn_in['bq'], 'L0_xattn_Wk': _L0_xattn_in['Wk'], 'L0_xattn_bk': _L0_xattn_in['bk'], 'L0_xattn_Wv': _L0_xattn_in['Wv'], 'L0_xattn_bv': _L0_xattn_in['bv'], 'L0_xattn_Wo': _L0_xattn_in['Wo'], 'L0_xattn_bo': _L0_xattn_in['bo'], 'L0_attn_Wq': _L0_attn_in['Wq'], 'L0_attn_bq': _L0_attn_in['bq'], 'L0_attn_Wk': _L0_attn_in['Wk'], 'L0_attn_bk': _L0_attn_in['bk'], 'L0_attn_Wv': _L0_attn_in['Wv'], 'L0_attn_bv': _L0_attn_in['bv'], 'L0_attn_Wo': _L0_attn_in['Wo'], 'L0_attn_bo': _L0_attn_in['bo'], 'L0_ffn_w_shared_in': _L0_ffn_in['w_shared_in'], 'L0_ffn_w_shared_out': _L0_ffn_in['w_shared_out'], 'L0_ffn_w1_shared': _L0_ffn_in['w1_shared'], 'L0_ffn_w2': _L0_ffn_in['w2'], 'L0_ffn_w_gate': _L0_ffn_in['w_gate'], 'L0_ffn_gate_bias': _L0_ffn_in['gate_bias']}

def reference(x, ctx_768, L0_xattn_Wq, L0_xattn_bq, L0_xattn_Wk, L0_xattn_bk, L0_xattn_Wv, L0_xattn_bv, L0_xattn_Wo, L0_xattn_bo, L0_attn_Wq, L0_attn_bq, L0_attn_Wk, L0_attn_bk, L0_attn_Wv, L0_attn_bv, L0_attn_Wo, L0_attn_bo, L0_ffn_w_shared_in, L0_ffn_w_shared_out, L0_ffn_w1_shared, L0_ffn_w2, L0_ffn_w_gate, L0_ffn_gate_bias):
    import jax
    import jax.numpy as jnp

    def _L0_xattn_ref(query, key_value, Wq, bq, Wk, bk, Wv, bv, Wo, bo):
        import jax, jax.numpy as jnp
        import numpy as np
        NUM_HEADS = 16
        CLAMP = 10000.0
        B, Nq, Cq = query.shape
        Nkv = key_value.shape[1]
        H = NUM_HEADS
        D = Cq // H
        scale = D ** (-0.5)
        q = (query @ Wq + bq).reshape(B, Nq, H, D).transpose(0, 2, 1, 3)
        k = (key_value @ Wk + bk).reshape(B, Nkv, H, D).transpose(0, 2, 1, 3)
        v = (key_value @ Wv + bv).reshape(B, Nkv, H, D).transpose(0, 2, 1, 3)
        attn = jnp.einsum('bhqd,bhkd->bhqk', q, k) * scale
        attn = jnp.clip(attn, -CLAMP, CLAMP)
        attn = jax.nn.softmax(attn, axis=-1)
        attn = jnp.where(jnp.any(jnp.isnan(attn)), jnp.asarray(1.0 / Nkv, attn.dtype), attn)
        x = jnp.einsum('bhqk,bhkd->bqhd', attn, v).reshape(B, Nq, Cq)
        return x @ Wo + bo

    def _L0_attn_ref(x, Wq, bq, Wk, bk, Wv, bv, Wo, bo):
        import jax, jax.numpy as jnp
        import numpy as np
        D_MODEL = 256
        NUM_HEADS = 16
        HEAD_DIM = D_MODEL // NUM_HEADS
        ALPHA = 1.0
        B, T, D = x.shape
        H, hd = (NUM_HEADS, HEAD_DIM)

        def split_heads(y):
            return y.reshape(B, T, H, hd).transpose(0, 2, 1, 3)
        Q = split_heads(x @ Wq.T + bq)
        K = split_heads(x @ Wk.T + bk)
        V = split_heads(x @ Wv.T + bv)
        scores = jnp.einsum('bhid,bhjd->bhij', Q, K) / jnp.sqrt(jnp.float32(hd))
        t = jnp.arange(T)
        delta = t[:, None] - t[None, :]
        causal_mask = delta < 0
        decay = jnp.where(causal_mask, 0.0, -delta.astype(jnp.float32) ** ALPHA)
        scores = jnp.where(causal_mask, -jnp.inf, scores) + decay
        attn = jax.nn.softmax(scores, axis=-1)
        out = jnp.einsum('bhij,bhjd->bhid', attn, V)
        out = out.transpose(0, 2, 1, 3).reshape(B, T, D)
        return out @ Wo.T + bo

    def _L0_ffn_ref(x, w_shared_in, w_shared_out, w1_shared, w2, w_gate, gate_bias):
        import jax, jax.numpy as jnp
        import numpy as np
        B, T, C, H, E, K = (4, 256, 256, 256, 8, 2)

        def _swiglu(x):
            a, b = jnp.split(x, 2, axis=-1)
            return jax.nn.silu(a) * b
        Bx, Tx, Cx = x.shape
        S = Bx * Tx
        fx = x.reshape(S, Cx)
        shared_out = _swiglu(fx @ w_shared_in) @ w_shared_out
        logits = fx @ w_gate + gate_bias
        probs = jax.nn.softmax(logits, axis=-1)
        top_val, top_idx = jax.lax.top_k(probs, K)
        wdense = jnp.zeros((S, E), probs.dtype).at[jnp.arange(S)[:, None], top_idx].add(top_val)
        hid = _swiglu(fx @ w1_shared)
        routed_out = jnp.zeros_like(shared_out)
        for e in range(E):
            routed_out = routed_out + wdense[:, e:e + 1] * (hid @ w2[e])
        return (shared_out + routed_out).reshape(Bx, Tx, Cx)
    x = x + _L0_xattn_ref(_layernorm(x, axis=-1), ctx_768, L0_xattn_Wq, L0_xattn_bq, L0_xattn_Wk, L0_xattn_bk, L0_xattn_Wv, L0_xattn_bv, L0_xattn_Wo, L0_xattn_bo)
    x = x + _L0_attn_ref(_layernorm(x, axis=-1), L0_attn_Wq, L0_attn_bq, L0_attn_Wk, L0_attn_bk, L0_attn_Wv, L0_attn_bv, L0_attn_Wo, L0_attn_bo)
    x = x + _L0_ffn_ref(_layernorm(x, axis=-1), L0_ffn_w_shared_in, L0_ffn_w_shared_out, L0_ffn_w1_shared, L0_ffn_w2, L0_ffn_w_gate, L0_ffn_gate_bias)
    return x

_drawn_inputs = setup_inputs


def setup_inputs(seed=0):
    import zlib

    import numpy as np

    out = dict(_drawn_inputs(seed))
    spreads = {'L0_xattn_bq': (0.0, 0.387),
     'L0_xattn_bk': (0.0, 0.8),
     'L0_xattn_bv': (0.0, 0.1),
     'L0_xattn_bo': (0.0, 0.1),
     'L0_ffn_gate_bias': (0.0, 0.8)}
    factors = {'L0_attn_bq': 8.0,
     'L0_attn_bk': 8.0,
     'L0_attn_bv': 3.323,
     'L0_ffn_w_shared_in': 3.935,
     'L0_ffn_w_shared_out': 3.96,
     'L0_ffn_w1_shared': 8.0,
     'L0_ffn_w2': 8.0,
     'L0_ffn_w_gate': 8.0}
    for name, (base, spread) in spreads.items():
        noise = np.random.default_rng([zlib.crc32(name.encode()), seed]).standard_normal(out[name].shape)
        drawn = base * np.exp(spread * noise) if base else spread * noise
        out[name] = jnp.asarray(drawn.astype(out[name].dtype))
    for name, factor in factors.items():
        out[name] = (out[name] * factor).astype(out[name].dtype)
    return out
```

```python
import concourse.bass as bass
from concourse import mybir
from contextlib import ExitStack

f32 = mybir.dt.float32
f32r = mybir.dt.float32r
ALU = mybir.AluOpType
ACT = mybir.ActivationFunctionType
AX = mybir.AxisListType

B, T, D = 64, 32, 256
S, C = 257, 192
H, HD = 16, 16
P = 128
TOK = B * T
NT = TOK // P
G = P // T
NG = B // G
HG = P // T
NHG = H // HG
DC = D // P
KT = 2
E, HID = 8, 256
SCALE = HD ** -0.5
CLAMP = 10000.0
EPS = 1e-5
LAST = S - 1
SP_ = S + 1
MASKED = -3.0e38


def perceiver_kernel(nc, x, ctx, xwq, xbq, xwk, xbk, xwv, xbv, xwo, xbo, awq, abq, awk, abk, awv, abv,
                     awo, abo, w_in, w_out, w1, w2, w_gate, gate_bias, out):
    stack = ExitStack()
    with stack:
        def sb(name, shape, dt=f32, on=stack):
            return on.enter_context(nc.sbuf_tensor(name, shape, dt))

        def sem(name, on=stack):
            return on.enter_context(nc.semaphore(name))

        pb = stack.enter_context(nc.psum_tensor("pb", [P, 8, 512], f32))
        ident = sb("ident", [P, P])
        head_mask = sb("head_mask", [P, 8])
        pair_mask = sb("pair_mask", [P, 2])
        X = sb("X", [P, NT, D])
        OT = sb("OT", [P, NT, DC, P])
        W2h = sb("W2h", [P, NG, D], f32r)
        W2l = sb("W2l", [P, NG, D], f32r)
        mean_var = sb("mean_var", [P, NT, 2])
        bnst = sb("bnst", [P, NT, 6])
        var_eps = sb("var_eps", [P, NT])
        rstd = sb("rstd", [P, NT])
        minus_half = sb("minus_half", [P, NT])

        def apart(eng):
            eng.nop(nofuse=True)


        cross = ExitStack()
        with cross:
            def sc(name, shape, dt=f32):
                return sb(name, shape, dt, cross)

            KVh = sc("KVh", [P, 2, 2, D], f32r)
            KVl = sc("KVl", [P, 2, 2, D], f32r)
            QTh = sc("QTh", [P, DC, TOK], f32r)
            QTl = sc("QTl", [P, DC, TOK], f32r)
            KL = sc("KL", [P, B, DC, 2], f32r)
            VL = sc("VL", [G, NG, D])
            bk = sc("bk", [P, DC])
            stacked_id = sc("stacked_id", [P, T])
            head_rows = sc("head_rows", [P, 2, P])

            pro = ExitStack()
            with pro:
                def sp0(name, shape, dt=f32):
                    return sb(name, shape, dt, pro)

                kvraw = sp0("kvraw", [P, 2, 2, D])
                wqraw = sp0("wqraw", [P, DC, D])
                WQh = sp0("WQh", [P, DC, D], f32r)
                WQl = sp0("WQl", [P, DC, D], f32r)
                bq = sp0("bq", [P, DC])
                xTh = sp0("xTh", [P, DC, TOK], f32r)
                xTl = sp0("xTl", [P, DC, TOK], f32r)
                qtmp = sp0("qtmp", [P, DC, 512])
                ctxl = sp0("ctxl", [B, C])
                CL = sp0("CL", [P, 3, B], f32r)
                VLa = sp0("VLa", [B, D])
                ones = sp0("ones", [P, P])
                hmt = sp0("hmt", [P, 8])
                hrt = sp0("hrt", [P, 4, 16])
                xn = OT[:].rearrange("p t c n -> p t (c n)")

                x_in = [sem(f"x_in{b}", pro) for b in range(4)]
                wq_in, kv_in, bias_in, cl_in = (sem(n, pro) for n in ("wq_in", "kv_in", "bias_in", "cl_in"))
                vl_in, consts, const_step = (sem(n, pro) for n in ("vl_in", "consts", "const_step"))
                stats, aggr, eps_added, rstd_ready, xn_ready = (
                    sem(n, pro) for n in ("stats", "aggr", "eps_added", "rstd_ready", "xn_ready"))
                xt_done, xt_hi, xt_lo, q_done, q_scaled, q_hi, q_lo = (
                    sem(n, pro) for n in ("xt_done", "xt_hi", "xt_lo", "q_done", "q_scaled", "q_hi", "q_lo"))
                wq_hi, wq_lo, kv_hi, kv_lo = (sem(n, pro) for n in ("wq_hi", "wq_lo", "kv_hi", "kv_lo"))
                cl_t, cl_hi, cl_lo, left_k, left_v, kl_hi, kl_lo, vl_out = (
                    sem(n, pro) for n in ("cl_t", "cl_hi", "cl_lo", "left_k", "left_v", "kl_hi", "kl_lo", "vl_out"))

                x_v = x.rearrange("b t d -> (b t) d").rearrange("(n p) d -> p n d", p=P)
                with nc.Block() as block:

                    @block.sync
                    def _(sp):
                        sp.dma_start(X[:, 0:4, :], x_v[:, 0:4, :]).then_inc(x_in[0], 16)
                        sp.dma_start(wqraw[:], xwq.rearrange("(c p) n -> p c n", p=P)).then_inc(wq_in, 16)
                        for b in range(1, 4):
                            sp.dma_start(X[:, 4 * b:4 * b + 4, :], x_v[:, 4 * b:4 * b + 4, :]).then_inc(x_in[b], 16)
                        sp.wait_ge(vl_out, 1)
                        for r in range(G):
                            sp.dma_start(VL[r:r + 1, :, :], VLa[r:B:G, :]).then_inc(vl_in, 16)
                        sp.wait_ge(vl_in, 16 * G)

                    @block.gpsimd
                    def _(pool):
                        with nc.allow_non_contiguous_dma(reason="biases, one element per partition"):
                            pool.dma_start(bq[:], xbq.rearrange("(c p) -> p c", p=P)).then_inc(bias_in, 16)
                            pool.dma_start(bk[:], xbk.rearrange("(c p) -> p c", p=P)).then_inc(bias_in, 16)
                        nc.gpsimd.memset(ident[:], 0.0)
                        nc.gpsimd.memset(ones[:], 1.0)
                        nc.gpsimd.memset(head_rows[:], 0.0)
                        nc.gpsimd.memset(minus_half[:], -0.5).then_inc(const_step, 1)
                        pool.wait_ge(const_step, 1)
                        nc.gpsimd.affine_select(out=ident[:], in_=ident[:], compare_op=ALU.not_equal, fill=1.0,
                                                base=0, pattern=[[-1, P]], channel_multiplier=1)
                        nc.gpsimd.affine_select(out=hmt[:], in_=ones[:, 0:8], compare_op=ALU.is_ge, fill=0.0,
                                                base=0, pattern=[[-HD, 8]], channel_multiplier=1)
                        nc.gpsimd.affine_select(out=hrt[:], in_=ones[:, 0:64].rearrange("p (h d) -> p h d", d=16),
                                                compare_op=ALU.is_ge, fill=0.0, base=0,
                                                pattern=[[-T, 4], [0, 16]], channel_multiplier=1).then_inc(const_step, 1)
                        pool.wait_ge(const_step, 2)
                        nc.gpsimd.affine_select(out=head_mask[:], in_=hmt[:], compare_op=ALU.is_ge, fill=0.0,
                                                base=HD - 1, pattern=[[HD, 8]], channel_multiplier=-1)
                        for par in range(2):
                            o = head_rows[:, par, 64 * par:64 * par + 64].rearrange("p (h d) -> p h d", d=16)
                            last = nc.gpsimd.affine_select(out=o, in_=hrt[:], compare_op=ALU.is_ge, fill=0.0,
                                                           base=T - 1, pattern=[[T, 4], [0, 16]], channel_multiplier=-1)
                        last.then_inc(consts, 1)
                        for b in range(4):
                            t = slice(4 * b, 4 * b + 4)
                            pool.wait_ge(aggr, b + 1)
                            nc.gpsimd.tensor_scalar(var_eps[:, t], mean_var[:, t, 1], EPS, None, ALU.add).then_inc(eps_added, 1)
                            pool.wait_ge(eps_added, b + 1)
                            nc.gpsimd.tensor_tensor(rstd[:, t], var_eps[:, t], minus_half[:, t], ALU.pow).then_inc(rstd_ready, 1)
                        for b in range(4):
                            for co in range(DC):
                                k = 2 * b + co + 1
                                pool.wait_ge(q_hi, k)
                                nc.gpsimd.tensor_tensor(QTl[:, co, 512 * b:512 * b + 512], qtmp[:, co, :],
                                                        QTh[:, co, 512 * b:512 * b + 512].bitcast(f32),
                                                        ALU.subtract).then_inc(q_lo, 1)

                    @block.scalar
                    def _(act):
                        act.dma_start(ctxl[:], ctx[:, LAST, :]).then_inc(cl_in, 16)
                        for k, w in enumerate((xwk, xwv)):
                            act.dma_start(kvraw[:, k, 0, :], w[0:P, :]).then_inc(kv_in, 16)
                            act.dma_start(kvraw[0:64, k, 1, :], w[P:C, :]).then_inc(kv_in, 16)
                            act.dma_start(kvraw[64:P, k, 1, :], w[P:C, :]).then_inc(kv_in, 16)
                        act.wait_ge(wq_in, 16)
                        nc.scalar.activation(WQh[:], wqraw[:], ACT.Copy).then_inc(wq_hi, 1)
                        act.wait_ge(kv_in, 96)
                        nc.scalar.activation(KVh[:], kvraw[:], ACT.Copy).then_inc(kv_hi, 1)
                        act.wait_ge(cl_t, 1)
                        nc.scalar.activation(CL[:, 0, :], pb[:, 6, 0:B], ACT.Copy)
                        nc.scalar.activation(CL[0:64, 2, :], pb[0:64, 6, B:2 * B], ACT.Copy).then_inc(cl_hi, 1)
                        act.wait_ge(bias_in, 32)
                        act.wait_ge(left_k, 1)
                        for c in range(DC):
                            last = nc.scalar.activation(KL[:, :, c, 0], pb[:, 7, c * B:c * B + B], ACT.Identity,
                                                        bias=bk[:, c:c + 1])
                        last.then_inc(kl_hi, 1)
                        act.wait_ge(left_v, 1)
                        nc.scalar.activation(VLa[:], pb[0:B, 6, 256:512], ACT.Copy).then_inc(vl_out, 1)
                        for b in range(4):
                            for c in range(DC):
                                act.wait_ge(xt_done, 2 * b + c + 1)
                                nc.scalar.activation(xTh[:, c, 512 * b:512 * b + 512], pb[:, 2 * (b % 2) + c, :],
                                                     ACT.Copy).then_inc(xt_hi, 1)
                            for co in range(DC):
                                act.wait_ge(q_scaled, 2 * b + co + 1)
                                nc.scalar.activation(QTh[:, co, 512 * b:512 * b + 512], qtmp[:, co, :],
                                                     ACT.Copy).then_inc(q_hi, 1)

                    @block.vector
                    def _(dve):
                        nc.vector.memset(KVl[64:P, :, 1, :].bitcast(f32), 0.0)
                        dve.wait_ge(wq_hi, 1)
                        nc.vector.tensor_tensor(WQl[:], wqraw[:], WQh[:].bitcast(f32), ALU.subtract).then_inc(wq_lo, 1)
                        for b in range(4):
                            dve.wait_ge(x_in[b], 16)
                            for t in range(4 * b, 4 * b + 4):
                                last = nc.vector.bn_stats(bnst[:, t, :], X[:, t, :])
                            last.then_inc(stats, 1)
                            dve.wait_ge(stats, b + 1)
                            for t in range(4 * b, 4 * b + 4):
                                last = nc.vector.bn_aggr(mean_var[:, t, :], bnst[:, t, :])
                            last.then_inc(aggr, 1)
                        dve.wait_ge(kv_hi, 1)
                        for k in range(2):
                            nc.vector.tensor_tensor(KVl[:, k, 0, :], kvraw[:, k, 0, :], KVh[:, k, 0, :].bitcast(f32), ALU.subtract)
                            last = nc.vector.tensor_tensor(KVl[0:64, k, 1, :], kvraw[0:64, k, 1, :],
                                                           KVh[0:64, k, 1, :].bitcast(f32), ALU.subtract)
                        last.then_inc(kv_lo, 1)
                        dve.wait_ge(cl_hi, 1)
                        nc.vector.tensor_tensor(CL[:, 1, :], pb[:, 6, 0:B], CL[:, 0, :].bitcast(f32), ALU.subtract)
                        nc.vector.tensor_tensor(CL[64:P, 2, :], pb[0:64, 6, B:2 * B], CL[0:64, 2, :].bitcast(f32),
                                                ALU.subtract).then_inc(cl_lo, 1)
                        for b in range(4):
                            dve.wait_ge(rstd_ready, b + 1)
                            for t in range(4 * b, 4 * b + 4):
                                last = nc.vector.tensor_scalar(xn[:, t, :], X[:, t, :], mean_var[:, t, 0:1],
                                                               rstd[:, t:t + 1], ALU.subtract, ALU.mult)
                            last.then_inc(xn_ready, 1)
                        dve.wait_ge(kl_hi, 1)
                        for c in range(DC):
                            last = nc.vector.scalar_tensor_tensor(KL[:, :, c, 1], pb[:, 7, c * B:c * B + B], bk[:, c:c + 1],
                                                                  KL[:, :, c, 0].bitcast(f32), ALU.add, ALU.subtract)
                        last.then_inc(kl_lo, 1)
                        dve.wait_ge(consts, 1)
                        nc.vector.tensor_reduce(pair_mask[:], head_mask[:].rearrange("p (j e) -> p e j", e=2), AX.X, ALU.add)
                        nc.vector.tensor_reduce(stacked_id[:], ident[:].rearrange("p (b q) -> p q b", q=T), AX.X, ALU.add)
                        dve.wait_ge(bias_in, 32)
                        for b in range(4):
                            for c in range(DC):
                                dve.wait_ge(xt_hi, 2 * b + c + 1)
                                nc.vector.tensor_tensor(xTl[:, c, 512 * b:512 * b + 512], pb[:, 2 * (b % 2) + c, :],
                                                        xTh[:, c, 512 * b:512 * b + 512].bitcast(f32),
                                                        ALU.subtract).then_inc(xt_lo, 1)
                            for co in range(DC):
                                dve.wait_ge(q_done, 2 * b + co + 1)
                                if b:
                                    dve.wait_ge(q_lo, 2 * b + co - 1)
                                nc.vector.tensor_scalar(qtmp[:, co, :], pb[:, 4 + co, :], bq[:, co:co + 1], SCALE,
                                                        ALU.add, ALU.mult).then_inc(q_scaled, 1)

                    @block.tensor
                    def _(pe):
                        pe.wait_ge(consts, 1)
                        pe.wait_ge(cl_in, 16)
                        nc.tensor.transpose(pb[:, 6, 0:B], ctxl[:, 0:P], ident[0:B, 0:B])
                        nc.tensor.transpose(pb[0:64, 6, B:2 * B], ctxl[:, P:C], ident[0:B, 0:B]).then_inc(cl_t, 1)
                        pe.wait_ge(kv_lo, 1)
                        pe.wait_ge(cl_lo, 1)
                        for c in range(DC):
                            cs = slice(c * P, c * P + P)
                            passes = ((KVh[:, 0, 0, cs], 0), (KVh[:, 0, 0, cs], 1), (KVl[:, 0, 0, cs], 0),
                                      (KVh[:, 0, 1, cs], 2), (KVl[:, 0, 1, cs], 2))
                            for m, (w, t) in enumerate(passes):
                                last = nc.tensor.matmul(pb[:, 7, c * B:c * B + B], w, CL[:, t, :], start=m == 0, stop=m == 4)
                        last.then_inc(left_k, 1)
                        passes = ((KVh[:, 1, 0, :], 0), (KVh[:, 1, 0, :], 1), (KVl[:, 1, 0, :], 0),
                                  (KVh[:, 1, 1, :], 2), (KVl[:, 1, 1, :], 2))
                        for m, (w, t) in enumerate(passes):
                            last = nc.tensor.matmul(pb[0:B, 6, 256:512], CL[:, t, :], w, start=m == 0, stop=m == 4)
                        last.then_inc(left_v, 1)

                        def project(b):
                            for c in range(DC):
                                pe.wait_ge(xt_lo, 2 * b + c + 1)
                            for co in range(DC):
                                if b:
                                    pe.wait_ge(q_scaled, 2 * b + co - 1)
                                cs = slice(co * P, co * P + P)
                                bs = slice(512 * b, 512 * b + 512)
                                for ci in range(DC):
                                    for m, (w, t) in enumerate(((WQh, xTh), (WQh, xTl), (WQl, xTh))):
                                        last = nc.tensor.matmul(pb[:, 4 + co, :], w[:, ci, cs], t[:, ci, bs],
                                                                start=(ci, m) == (0, 0), stop=(ci, m) == (1, 2))
                                last.then_inc(q_done, 1)

                        pe.wait_ge(wq_lo, 1)
                        for b in range(4):
                            pe.wait_ge(xn_ready, b + 1)
                            for c in range(DC):
                                if b >= 2:
                                    pe.wait_ge(xt_lo, 2 * (b - 2) + c + 1)
                                for t in range(4):
                                    last = nc.tensor.transpose(pb[:, 2 * (b % 2) + c, P * t:P * t + P],
                                                               xn[:, 4 * b + t, c * P:c * P + P], ident[:])
                                last.then_inc(xt_done, 1)
                            if b:
                                project(b - 1)
                        project(3)

            CX = [sc(f"CX{k}", [P, KT, C]) for k in range(4)]
            TR = [sc(f"TR{k}", [P, 3, KT * P], f32r) for k in range(2)]
            KR = [sc(f"KR{k}", [P, DC, 2, SP_], f32r) for k in range(2)]
            VR = [sc(f"VR{k}", [P, KT, D]) for k in range(2)]
            QB = [sc(f"QB{k}", [P, 2, DC, 8, T], f32r) for k in range(2)]
            SC = [sc(f"SC{k}", [P, NHG, S]) for k in range(2)]
            PR = sc("PR", [P, NHG, S])
            PTs = sc("PTs", [P, KT, NHG * P])
            PL = sc("PL", [P, NHG, G])
            PLT = sc("PLT", [G, NHG * P])
            VLm = sc("VLm", [G, G, D])
            neg_max = [sc(f"neg_max{k}", [P, NHG]) for k in range(2)]
            sums = sc("sums", [P, NHG, G])
            recip = sc("recip", [P, NHG, G])
            RST = sc("RST", [P, NHG * G, T])
            even_part = sc("even_part", [P, DC * G, T])
            both_parts = sc("both_parts", [P, DC * G, T])
            w2raw = sc("w2raw", [P, D])

            ctx_in = [sem(f"ctx_in{k}", cross) for k in range(4)]
            names = ("t_done", "t_hi", "t_lo", "k_done", "k_hi", "k_lo", "qk_ready", "v_done", "v_evac", "s_done",
                     "clipped", "neg_max_ready", "exp_done", "pl_copied", "vl_ready", "pt_done", "pt_evac",
                     "plt_done", "plt_evac", "pv_done", "pvl_done", "recip_done", "rst_ready", "rt_done", "even_done",
                     "both_done", "o_free", "w2_in", "w2_hi", "w2_lo", "pads")
            (t_done, t_hi, t_lo, k_done, k_hi, k_lo, qk_ready, v_done, v_evac, s_done, clipped,
             neg_max_ready, exp_done, pl_copied, vl_ready, pt_done, pt_evac, plt_done, plt_evac, pv_done, pvl_done,
             recip_done, rst_ready, rt_done, even_done, both_done, o_free, w2_in, w2_hi, w2_lo,
             pads) = (sem(n, cross) for n in names)
            psT, psK, psV, psS, psO, psM = pb[:, 0, :], (pb[:, 1, :], pb[:, 2, :]), pb[:, 3, :], (pb[:, 4, :], pb[:, 5, :]), pb[:, 6, :], pb[:, 7, :]
            ctx_v = ctx[:, 0:KT * P, :].rearrange("b (p t) c -> b p t c", t=KT)
            w2_v = w2.rearrange("e (c p) n -> (e c) p n", p=P)

            def over_groups(eng, step):
                for j in range(G):
                    step(0, j, j, False)
                with eng.Fori(1, NG - 1) as i:
                    for j in range(G):
                        step(i, j, i * G + j, False)
                for j in range(G):
                    step(NG - 1, j, (NG - 1) * G + j, True)

            with nc.Block() as block:

                @block.sync
                def _(sp):
                    def load(n, k):
                        src = ctx_v[n] if isinstance(n, int) else ctx_v[bass.ds(n, 1)].rearrange("a p t c -> p (a t) c")
                        sp.dma_start(CX[k][:], src).then_inc(ctx_in[k], 16)

                    for k in range(4):
                        load(k, k)

                    def step(i, j, n, last):
                        if not last:
                            sp.wait_ge(t_done, n + 1)
                            load(n + 4, j)
                        if j == 0:
                            sp.wait_ge(w2_lo, i)
                            src = w2_v[i] if isinstance(i, int) else w2_v[bass.ds(i, 1)].rearrange("a p n -> p (a n)")
                            sp.dma_start(w2raw[:], src).then_inc(w2_in, 16)

                    over_groups(sp, step)

                @block.gpsimd
                def _(pool):
                    for k in range(2):
                        last_i = nc.gpsimd.memset(KR[k][:, :, :, S:SP_].bitcast(f32), 0.0)
                    last_i.then_inc(pads, 1)

                    def keys_queries(n, k, first):
                        if not first:
                            pool.wait_ge(s_done, (n - 1) * 4)
                        for part, q in enumerate((QTh, QTl)):
                            src = q[:, :, bass.ds(n * T, T)].bitcast(f32).unsqueeze(2).broadcast_to([P, DC, 8, T])
                            msk = head_mask[:].unsqueeze(1).unsqueeze(3).broadcast_to([P, DC, 8, T])
                            nc.gpsimd.tensor_tensor(QB[k][:, part], src, msk, ALU.mult)
                        src = KL[:, bass.ds(n, 1), :, :].bitcast(f32).rearrange("p a c h -> p (a c) h").unsqueeze(3)
                        nc.gpsimd.tensor_copy(KR[k][:, :, :, LAST:S], src).then_inc(qk_ready, 1)

                    keys_queries(0, 0, True)

                    def step(i, j, n, last):
                        if not (last and j == G - 1):
                            keys_queries(n + 1, (j + 1) % 2, False)
                        pool.wait_ge(exp_done, (n + 1) * 4)
                        if j == 0:
                            pool.wait_ge(plt_done, i)
                        apart(pool)
                        nc.gpsimd.tensor_copy(PL[:, :, j], PR[:, :, LAST]).then_inc(pl_copied, 1)
                        if j == 1:
                            pool.wait_ge(pvl_done, i)
                            src = VL[:, bass.ds(i, 1), :].broadcast_to([G, G, D])
                            msk = ident[0:G, 0:G].unsqueeze(2).broadcast_to([G, G, D])
                            nc.gpsimd.tensor_tensor(VLm[:], src, msk, ALU.mult).then_inc(vl_ready, 1)

                    over_groups(pool, step)

                @block.scalar
                def _(act):
                    def context_hi(n, k, first):
                        act.wait_ge(t_done, n + 1)
                        if not first:
                            act.wait_ge(k_done, (n - 1) * 2)
                        nc.scalar.activation(TR[k][:, 0, :], psT[:, 0:KT * P], ACT.Copy)
                        nc.scalar.activation(TR[k][0:64, 2, :], psT[0:64, KT * P:2 * KT * P], ACT.Copy).then_inc(t_hi, 1)

                    def keys_hi(n, k, first):
                        if not first:
                            act.wait_ge(s_done, (n - 1) * 4)
                        for c in range(DC):
                            act.wait_ge(k_done, n * 2 + c + 1)
                            nc.scalar.activation(KR[k][:, c, 0, 0:LAST], psK[c][:, 0:LAST], ACT.Identity,
                                                 bias=bk[:, c:c + 1]).then_inc(k_hi, 1)

                    def values(n, k, first):
                        act.wait_ge(v_done, n + 1)
                        if not first:
                            act.wait_ge(pv_done, n - 1)
                        nc.scalar.activation(VR[k][:], psV[:, :], ACT.Copy).then_inc(v_evac, 1)

                    context_hi(0, 0, True)
                    context_hi(1, 1, True)
                    keys_hi(0, 0, True)
                    values(0, 0, True)

                    def step(i, j, n, last):
                        act.wait_ge(neg_max_ready, n + 1)
                        act.wait_ge(pt_done, n * 2)
                        act.wait_ge(pl_copied, n)
                        if j == 0:
                            act.wait_ge(recip_done, i)
                        for g in range(NHG):
                            nc.scalar.activation(PR[:, g, :], SC[j % 2][:, g, :], ACT.Exp, bias=neg_max[j % 2][:, g:g + 1],
                                                 accum_out=sums[:, g, j:j + 1]).then_inc(exp_done, 1)
                            if g == 0 and not (last and j == G - 1):
                                keys_hi(n + 1, (j + 1) % 2, False)
                            if g == 1 and not (last and j >= G - 2):
                                context_hi(n + 2, j % 2, False)
                        if not (last and j == G - 1):
                            values(n + 1, (j + 1) % 2, False)
                        if j == 1:
                            act.wait_ge(w2_in, i * 16 + 16)
                            nc.scalar.activation(W2h[:, bass.ds(i, 1), :], w2raw[:].unsqueeze(1), ACT.Copy).then_inc(w2_hi, 1)
                        act.wait_ge(pv_done, n)
                        for kt in range(KT):
                            act.wait_ge(pt_done, n * 2 + kt + 1)
                            nc.scalar.activation(PTs[:, kt, :], psK[kt], ACT.Copy).then_inc(pt_evac, 1)
                        if j == G - 1:
                            act.wait_ge(plt_done, i + 1)
                            act.wait_ge(pvl_done, i)
                            nc.scalar.activation(PLT[:], psM[0:G, :], ACT.Copy).then_inc(plt_evac, 1)

                    over_groups(act, step)

                @block.vector
                def _(dve):
                    def context_lo(n, k):
                        dve.wait_ge(t_hi, n + 1)
                        nc.vector.tensor_tensor(TR[k][:, 1, :], psT[:, 0:KT * P], TR[k][:, 0, :].bitcast(f32), ALU.subtract)
                        nc.vector.tensor_tensor(TR[k][64:P, 2, :], psT[0:64, KT * P:2 * KT * P],
                                                TR[k][0:64, 2, :].bitcast(f32), ALU.subtract).then_inc(t_lo, 1)

                    def keys_lo(n, k):
                        for c in range(DC):
                            dve.wait_ge(k_hi, n * 2 + c + 1)
                            nc.vector.scalar_tensor_tensor(KR[k][:, c, 1, 0:LAST], psK[c][:, 0:LAST], bk[:, c:c + 1],
                                                           KR[k][:, c, 0, 0:LAST].bitcast(f32),
                                                           ALU.add, ALU.subtract).then_inc(k_lo, 1)

                    def clip(n, k, c):
                        if c == 0 and (not isinstance(n, int) or n > 1):
                            dve.wait_ge(exp_done, (n - 1) * 4)
                        for g in (2 * c, 2 * c + 1):
                            dve.wait_ge(s_done, n * 4 + g + 1)
                            nc.vector.tensor_scalar(SC[k][:, g, :], psS[g % 2][:, 0:S], CLAMP, -CLAMP,
                                                    ALU.min, ALU.max).then_inc(clipped, 1)

                    def row_max(n, k):
                        dve.wait_ge(clipped, n * 4 + 4)
                        nc.vector.tensor_reduce(neg_max[k][:], SC[k][:], AX.X, ALU.max, negate=True).then_inc(neg_max_ready, 1)

                    def finish(i):
                        o = psO.rearrange("p (cb e q) -> p cb e q", e=2, q=T)
                        dve.wait_ge(rt_done, i + 1)
                        dve.wait_ge(pv_done, i * G + G)
                        nc.vector.tensor_scalar(even_part[:], o[:, :, 0, :], pair_mask[:, 0:1], None, ALU.mult).then_inc(even_done, 1)
                        dve.wait_ge(even_done, i + 1)
                        nc.vector.scalar_tensor_tensor(both_parts[:], o[:, :, 1, :], pair_mask[:, 1:2], even_part[:],
                                                       ALU.mult, ALU.add).then_inc(both_done, 1)
                        dve.wait_ge(both_done, i + 1)
                        nc.vector.tensor_tensor(OT[:, bass.ds(i, 1), :, :].rearrange("p a c t -> p (a c) t"),
                                                both_parts[:].rearrange("p (c b) q -> p c (b q)", c=DC),
                                                psM[:, 0:DC * P].rearrange("p (c t) -> p c t", c=DC),
                                                ALU.mult).then_inc(o_free, 1)

                    context_lo(0, 0)
                    context_lo(1, 1)
                    keys_lo(0, 0)
                    for c in range(DC):
                        clip(0, 0, c)
                    row_max(0, 0)

                    def step(i, j, n, last):
                        if not (last and j == G - 1):
                            keys_lo(n + 1, (j + 1) % 2)
                            clip(n + 1, (j + 1) % 2, 0)
                        if not (last and j >= G - 2):
                            context_lo(n + 2, j % 2)
                        if not (last and j == G - 1):
                            clip(n + 1, (j + 1) % 2, 1)
                        if j == G - 1:
                            dve.wait_ge(exp_done, (n + 1) * 4)
                            nc.vector.reciprocal(recip[:], sums[:]).then_inc(recip_done, 1)
                        if not (last and j == G - 1):
                            row_max(n + 1, (j + 1) % 2)
                        if j == 0 and not (isinstance(i, int) and i == 0):
                            finish(i - 1)
                        if j == 1:
                            dve.wait_ge(w2_hi, i + 1)
                            nc.vector.tensor_tensor(W2l[:, bass.ds(i, 1), :], w2raw[:].unsqueeze(1),
                                                    W2h[:, bass.ds(i, 1), :].bitcast(f32), ALU.subtract).then_inc(w2_lo, 1)
                        if j == G - 1:
                            dve.wait_ge(recip_done, i + 1)
                            dve.wait_ge(rt_done, i)
                            nc.vector.tensor_tensor(RST[:], stacked_id[:].unsqueeze(1).broadcast_to([P, NHG * G, T]),
                                                    recip[:].rearrange("p g b -> p (g b)").unsqueeze(2).broadcast_to([P, NHG * G, T]),
                                                    ALU.mult).then_inc(rst_ready, 1)

                    over_groups(dve, step)
                    finish(NG - 1)

                @block.tensor
                def _(pe):
                    def transpose_context(n, k, slot, first):
                        pe.wait_ge(ctx_in[slot], (n // 4) * 16 + 16 if isinstance(n, int) else k)
                        if not first:
                            pe.wait_ge(t_lo, n)
                        for t in range(KT):
                            nc.tensor.transpose(psT[:, P * t:P * t + P], CX[slot][:, t, 0:P], ident[:])
                        for t in range(KT):
                            last_i = nc.tensor.transpose(psT[0:64, KT * P + P * t:KT * P + P * t + P], CX[slot][:, t, P:C], ident[:])
                        last_i.then_inc(t_done, 1)

                    def values(n, k, first):
                        pe.wait_ge(t_lo, n + 1)
                        if not first:
                            pe.wait_ge(v_evac, n)
                        passes = ((KVh[:, 1, 0, :], 0), (KVh[:, 1, 0, :], 1), (KVl[:, 1, 0, :], 0),
                                  (KVh[:, 1, 1, :], 2), (KVl[:, 1, 1, :], 2))
                        for kt in range(KT):
                            for m, (w, t) in enumerate(passes):
                                last_i = nc.tensor.matmul(psV[:, D * kt:D * kt + D], TR[k][:, t, P * kt:P * kt + P], w,
                                                          start=m == 0, stop=m == 4)
                        last_i.then_inc(v_done, 1)

                    def keys(n, k, first):
                        if not first:
                            pe.wait_ge(pt_evac, (n - 1) * 2)
                        for c in range(DC):
                            cs = slice(c * P, c * P + P)
                            passes = ((KVh[:, 0, 0, cs], 0), (KVh[:, 0, 0, cs], 1), (KVl[:, 0, 0, cs], 0),
                                      (KVh[:, 0, 1, cs], 2), (KVl[:, 0, 1, cs], 2))
                            for m, (w, t) in enumerate(passes):
                                last_i = nc.tensor.matmul(psK[c][:, 0:LAST], w, TR[k][:, t, :], start=m == 0, stop=m == 4)
                            last_i.then_inc(k_done, 1)

                    def scores(n, k, c, first):
                        pe.wait_ge(k_lo, n * 2 + c + 1)
                        if c == 0:
                            pe.wait_ge(qk_ready, n + 1)
                        for g in (2 * c, 2 * c + 1):
                            if not (first and g < 2):
                                pe.wait_ge(clipped, n * 4 + g - 1)
                            gs = slice(4 * (g % 2), 4 * (g % 2) + 4)
                            q = [QB[k][:, part, c, gs, :].rearrange("p h q -> p (h q)") for part in range(2)]
                            for m, (a, b) in enumerate(((0, 0), (0, 1), (1, 0))):
                                last_i = nc.tensor.matmul(psS[g % 2][:, 0:SP_], q[a], KR[k][:, c, b, :], start=m == 0, stop=m == 2)
                            last_i.then_inc(s_done, 1)

                    def weigh(n, i, j, kt):
                        if kt == 0:
                            if j == 0:
                                pe.wait_ge(o_free, i)
                            pe.wait_ge(v_evac, n + 1)
                        pe.wait_ge(pt_evac, n * 2 + kt + 1)
                        for c in range(DC):
                            o = (c * G + j) * 64
                            for jj in range(4):
                                r = slice(32 * jj, 32 * jj + 32)
                                last_i = nc.tensor.matmul(psO[r, o:o + 64], VR[j % 2][:, kt, c * P + 32 * jj:c * P + 32 * jj + 32],
                                                          PTs[:, kt, (c * 4 + jj) * 64:(c * 4 + jj) * 64 + 64],
                                                          start=(j, kt, c) == (0, 0, 0),
                                                          stop=(j, kt, c) == (G - 1, KT - 1, DC - 1), skip_group_check=True)
                        if kt == KT - 1:
                            last_i.then_inc(pv_done, 1)

                    pe.wait_ge(pads, 1)
                    transpose_context(0, None, 0, True)
                    transpose_context(1, None, 1, False)
                    values(0, 0, True)
                    keys(0, 0, True)
                    for c in range(DC):
                        scores(0, 0, c, True)

                    def finish(i):
                        pe.wait_ge(plt_evac, i + 1)
                        pe.wait_ge(vl_ready, i + 1)
                        apart(pe)
                        for b in range(G):
                            for c in range(DC):
                                o = (c * G + b) * 64
                                for jj in range(4):
                                    r = slice(32 * jj, 32 * jj + 32)
                                    last_i = nc.tensor.matmul(psO[r, o:o + 64], VLm[:, b, c * P + 32 * jj:c * P + 32 * jj + 32],
                                                              PLT[:, (c * 4 + jj) * 64:(c * 4 + jj) * 64 + 64],
                                                              start=False, stop=False, skip_group_check=True)
                        last_i.then_inc(pvl_done, 1)
                        pe.wait_ge(rst_ready, i + 1)
                        for c in range(DC):
                            for par in range(2):
                                g = 2 * c + par
                                last_i = nc.tensor.matmul(psM[:, P * c:P * c + P], head_rows[:, par, :],
                                                          RST[:, G * g:G * g + G, :].rearrange("p b q -> p (b q)"),
                                                          start=par == 0, stop=par == 1)
                        last_i.then_inc(rt_done, 1)

                    def step(i, j, n, last):
                        if not (last and j == G - 1):
                            values(n + 1, (j + 1) % 2, False)
                            keys(n + 1, (j + 1) % 2, False)
                        if not (last and j >= G - 2):
                            transpose_context(n + 2, i * 16 + 16 * ((j + 2) // 4) + 16, (j + 2) % 4, False)
                        if j == 0 and not (isinstance(i, int) and i == 0):
                            finish(i - 1)
                        before = (n - 1, i if j else i - 1, (j - 1) % G)
                        for c in range(DC):
                            if j or not (isinstance(i, int) and i == 0):
                                weigh(*before, c)
                            if not (last and j == G - 1):
                                scores(n + 1, (j + 1) % 2, c, False)
                        pe.wait_ge(exp_done, (n + 1) * 4)
                        for kt in range(KT):
                            for g in range(NHG):
                                last_i = nc.tensor.transpose(psK[kt][:, P * g:P * g + P], PR[:, g, P * kt:P * kt + P], ident[:])
                            last_i.then_inc(pt_done, 1)
                        if j == G - 1:
                            pe.wait_ge(pl_copied, (n + 1))
                            pe.wait_ge(o_free, i)
                            for g in range(NHG):
                                last_i = nc.tensor.transpose(psM[0:G, P * g:P * g + P], PL[:, g, :], ident[:])
                            last_i.then_inc(plt_done, 1)

                    over_groups(pe, step)
                    finish(NG - 1)
                    for kt in range(KT):
                        weigh(B - 1, NG - 1, G - 1, kt)

        XWOh, XWOl = sb("XWOh", [P, DC, D], f32r), sb("XWOl", [P, DC, D], f32r)
        AWh, AWl = sb("AWh", [P, 4, DC, D], f32r), sb("AWl", [P, 4, DC, D], f32r)
        WIh, WIl = sb("WIh", [P, DC, 2, 2 * HID], f32r), sb("WIl", [P, DC, 2, 2 * HID], f32r)
        WSh, WSl = sb("WSh", [P, DC, D], f32r), sb("WSl", [P, DC, D], f32r)
        WGh, WGl = sb("WGh", [P, DC, E], f32r), sb("WGl", [P, DC, E], f32r)
        bias_rows = sb("bias_rows", [64, 2, D], f32r)
        ones_row = sb("ones_row", [64, P], f32r)
        bcol = sb("bcol", [P, 4, DC])
        gate_b = sb("gate_b", [P, E])
        decay = sb("decay", [P, T])
        QT = sb("QT", [P, DC, TOK])
        KTm = sb("KTm", [P, DC, TOK])
        V = OT[:].rearrange("p t c n -> p t (c n)")

        setup = ExitStack()
        with setup:
            xwo_raw = sb("xwo_raw", [P, DC, D], f32, setup)
            aw_raw = sb("aw_raw", [P, 4, DC, D], f32, setup)
            wi_raw = sb("wi_raw", [P, DC, 2, 2 * HID], f32, setup)
            ws_raw = sb("ws_raw", [P, DC, D], f32, setup)
            wg_raw = sb("wg_raw", [P, DC, E], f32, setup)
            brow_raw = sb("brow_raw", [33, 2, D], f32, setup)
            brow_hi = sb("brow_hi", [33, 2, D], f32r, setup)
            ii = sb("ii", [P, G, T], mybir.dt.int32, setup)
            dist = [sb(f"dist{k}", [P, G, T], f32, setup) for k in range(4)]
            sem_in = {n: sem(n, setup) for n in ("xwo_in", "aw_in", "wi_in", "ws_in", "wg_in", "br_in", "bc_in")}
            dist_step, decay_ready, awt_done = sem("dist_step", setup), sem("decay_ready", setup), sem("awt_done", setup)
            br_zero, br_hi, set_hi, set_lo = (sem(n, setup) for n in ("br_zero", "br_hi", "set_hi", "set_lo"))
            set_pool = sem("set_pool", setup)
            with nc.Block() as block:

                @block.sync
                def _(sp):
                    for k, w in enumerate((awq, awk, awv, awo)):
                        sp.dma_start(aw_raw[:, k], w.rearrange("(o p) n -> p o n", p=P)).then_inc(sem_in["aw_in"], 16)
                    for k, w in enumerate((w_in, w1)):
                        sp.dma_start(wi_raw[:, :, k, :], w.rearrange("(c p) n -> p c n", p=P)).then_inc(sem_in["wi_in"], 16)
                    sp.dma_start(ws_raw[:], w_out.rearrange("(c p) n -> p c n", p=P)).then_inc(sem_in["ws_in"], 16)
                    sp.dma_start(wg_raw[:], w_gate.rearrange("(c p) n -> p c n", p=P)).then_inc(sem_in["wg_in"], 16)

                @block.scalar
                def _(act):
                    act.dma_start(xwo_raw[:], xwo.rearrange("(c p) n -> p c n", p=P)).then_inc(sem_in["xwo_in"], 16)
                    for k, b in enumerate((xbo, abo)):
                        for r in (0, 32):
                            act.dma_start(brow_raw[r:r + 1, k, :], b.rearrange("(a n) -> a n", a=1)).then_inc(sem_in["br_in"], 16)
                    with nc.allow_non_contiguous_dma(reason="biases, one element per partition"):
                        for k, b in enumerate((xbv, abq, abk, abv)):
                            act.dma_start(bcol[:, k, :], b.rearrange("(c p) -> p c", p=P)).then_inc(sem_in["bc_in"], 16)
                    act.dma_start(gate_b[:], gate_bias.rearrange("(a n) -> a n", a=1).broadcast_to([P, E])).then_inc(sem_in["bc_in"], 16)
                    act.wait_ge(sem_in["xwo_in"], 16)
                    nc.scalar.activation(XWOh[:], xwo_raw[:], ACT.Copy).then_inc(set_hi, 1)
                    act.wait_ge(sem_in["br_in"], 64)
                    act.wait_ge(br_zero, 1)
                    nc.scalar.activation(bias_rows[0:1], brow_raw[0:1], ACT.Copy)
                    nc.scalar.activation(brow_hi[32:33], brow_raw[32:33], ACT.Copy).then_inc(br_hi, 1)
                    for k in range(4):
                        act.wait_ge(awt_done, k + 1)
                        nc.scalar.activation(AWh[:, k], pb[:, k, :].rearrange("p (c n) -> p c n", c=DC), ACT.Copy).then_inc(set_hi, 1)
                    act.wait_ge(sem_in["wi_in"], 32)
                    nc.scalar.activation(WIh[:], wi_raw[:], ACT.Copy).then_inc(set_hi, 1)
                    act.wait_ge(sem_in["ws_in"], 16)
                    nc.scalar.activation(WSh[:], ws_raw[:], ACT.Copy).then_inc(set_hi, 1)
                    act.wait_ge(sem_in["wg_in"], 16)
                    nc.scalar.activation(WGh[:], wg_raw[:], ACT.Copy).then_inc(set_hi, 1)
                    act.wait_ge(sem_in["bc_in"], 80)

                @block.vector
                def _(dve):
                    nc.vector.memset(ones_row[:].bitcast(f32), 1.0)
                    nc.vector.memset(bias_rows[:].bitcast(f32), 0.0).then_inc(br_zero, 1)
                    dve.wait_ge(set_hi, 1)
                    nc.vector.tensor_tensor(XWOl[:], xwo_raw[:], XWOh[:].bitcast(f32), ALU.subtract)
                    dve.wait_ge(br_hi, 1)
                    nc.vector.tensor_tensor(bias_rows[32:33], brow_raw[32:33], brow_hi[32:33].bitcast(f32), ALU.subtract)
                    for k in range(4):
                        dve.wait_ge(set_hi, k + 2)
                        nc.vector.tensor_tensor(AWl[:, k], pb[:, k, :].rearrange("p (c n) -> p c n", c=DC),
                                                AWh[:, k].bitcast(f32), ALU.subtract)
                    dve.wait_ge(set_hi, 7)
                    nc.vector.tensor_tensor(WSl[:], ws_raw[:], WSh[:].bitcast(f32), ALU.subtract)
                    dve.wait_ge(set_hi, 8)
                    nc.vector.tensor_tensor(WGl[:], wg_raw[:], WGh[:].bitcast(f32), ALU.subtract).then_inc(set_lo, 1)
                    dve.wait_ge(decay_ready, 1)
                    nc.vector.tensor_reduce(decay[:], dist[3][:].rearrange("p b k -> p k b"), AX.X, ALU.add)

                @block.gpsimd
                def _(pool):
                    nc.gpsimd.iota(ii[:], pattern=[[T, G], [1, T]], base=0, channel_multiplier=-1).then_inc(dist_step, 1)
                    pool.wait_ge(dist_step, 1)
                    nc.gpsimd.tensor_copy(dist[0][:], ii[:]).then_inc(dist_step, 1)
                    pool.wait_ge(dist_step, 2)
                    nc.gpsimd.affine_select(out=dist[1][:], in_=dist[0][:], compare_op=ALU.is_ge, fill=MASKED, base=0,
                                            pattern=[[-T, G], [-1, T]], channel_multiplier=1).then_inc(dist_step, 1)
                    pool.wait_ge(dist_step, 3)
                    nc.gpsimd.affine_select(out=dist[2][:], in_=dist[1][:], compare_op=ALU.is_ge, fill=0.0, base=0,
                                            pattern=[[-T, G], [0, T]], channel_multiplier=1).then_inc(dist_step, 1)
                    pool.wait_ge(dist_step, 4)
                    nc.gpsimd.affine_select(out=dist[3][:], in_=dist[2][:], compare_op=ALU.is_ge, fill=0.0, base=T - 1,
                                            pattern=[[T, G], [0, T]], channel_multiplier=-1).then_inc(decay_ready, 1)
                    pool.wait_ge(set_hi, 6)
                    nc.gpsimd.tensor_tensor(WIl[:], wi_raw[:], WIh[:].bitcast(f32), ALU.subtract).then_inc(set_pool, 1)

                @block.tensor
                def _(pe):
                    for k in range(4):
                        pe.wait_ge(sem_in["aw_in"], 64)
                        for ic in range(DC):
                            for oc in range(DC):
                                last = nc.tensor.transpose(pb[:, k, ic * D + oc * P:ic * D + oc * P + P],
                                                           aw_raw[:, k, oc, ic * P:ic * P + P], ident[:])
                        last.then_inc(awt_done, 1)

        def split_mm(o, pairs, start=True, stop=True):
            n = len(pairs)
            for a, (lhs, rhs) in enumerate(pairs):
                for m, (p, q) in enumerate(((0, 0), (0, 1), (1, 0))):
                    last = nc.tensor.matmul(o, lhs[p], rhs[q], start=start and (a, m) == (0, 0), stop=stop and (a, m) == (n - 1, 2))
            return last

        NB = 4
        BW = TOK // NB
        blk = ExitStack()
        with blk:
            oh, ol = sb("oh", [P, DC, BW], f32r, blk), sb("ol", [P, DC, BW], f32r, blk)
            bh, bl = sb("bh", [P, DC, BW], f32r, blk), sb("bl", [P, DC, BW], f32r, blk)
            bq4 = sb("bq4", [P, DC], f32, blk)
            xnb = sb("xnb", [P, 4, D], f32, blk)
            st = sb("st", [P, 4, 6], f32, blk)
            mv = sb("mv", [P, 4, 2], f32, blk)
            ve = sb("ve", [P, 4], f32, blk)
            rs = sb("rs", [P, 4], f32, blk)
            (o_hi, o_lo, y_done, x1_ready, st_ready, mv_ready, ve_ready, rs_ready, xn_done, tr_done, tr_hi, tr_lo,
             p_done, p_evac, bq4_ready) = (sem("a_" + n, blk) for n in (
                 "o_hi", "o_lo", "y_done", "x1_ready", "st_ready", "mv_ready", "ve_ready", "rs_ready", "xn_done",
                 "tr_done", "tr_hi", "tr_lo", "p_done", "p_evac", "bq4_ready"))
            with nc.Block() as block:

                def over_blocks(eng, step):
                    step(0, True)
                    with eng.Fori(1, NB) as k:
                        step(k, False)

                @block.scalar
                def _(act):
                    def split_o(k):
                        act.wait_ge(y_done, k * 4)
                        for c in range(DC):
                            nc.scalar.activation(oh[:, c, :].rearrange("p (t n) -> p t n", n=P), OT[:, bass.ds(k * 4, 4), c, :], ACT.Identity,
                                                 bias=bcol[:, 0, c:c + 1]).then_inc(o_hi, 1)

                    def evacuate(k):
                        act.wait_ge(bq4_ready, 1)
                        for m in range(6):
                            act.wait_ge(p_done, k * 6 + m + 1)
                            src = pb[:, 6 + m % 2, :]
                            if m < 2:
                                last = nc.scalar.activation(QT[:, m, bass.ds(k * BW, BW)], src, ACT.Identity,
                                                            bias=bq4[:, m:m + 1], scale=SCALE)
                            elif m < 4:
                                last = nc.scalar.activation(KTm[:, m - 2, bass.ds(k * BW, BW)], src, ACT.Identity,
                                                            bias=bcol[:, 2, m - 2:m - 1])
                            else:
                                last = nc.scalar.activation(V[:, bass.ds(k * 4 + (m - 4) * 2, 2), :],
                                                            src.rearrange("p (t n) -> p t n", n=D), ACT.Copy)
                            last.then_inc(p_evac, 1)

                    def step(k, first):
                        split_o(k)
                        if not first:
                            evacuate(k - 1)
                        for c in range(DC):
                            act.wait_ge(tr_done, k * 2 + c + 1)
                            if c == 0:
                                act.wait_ge(p_done, k * 6)
                            nc.scalar.activation(bh[:, c, :], pb[:, 4 + c, :], ACT.Copy).then_inc(tr_hi, 1)

                    over_blocks(act, step)
                    evacuate(NB - 1)

                @block.vector
                def _(dve):
                    nc.vector.tensor_scalar(bq4[:], bcol[:, 1, :], SCALE, None, ALU.mult).then_inc(bq4_ready, 1)

                    def step(k, first):
                        for c in range(DC):
                            dve.wait_ge(o_hi, k * 2 + c + 1)
                            nc.vector.scalar_tensor_tensor(ol[:, c, :].rearrange("p (t n) -> p t n", n=P), OT[:, bass.ds(k * 4, 4), c, :],
                                                           bcol[:, 0, c:c + 1], oh[:, c, :].bitcast(f32).rearrange("p (t n) -> p t n", n=P),
                                                           ALU.add, ALU.subtract).then_inc(o_lo, 1)
                        for t in range(4):
                            dve.wait_ge(y_done, k * 4 + t + 1)
                            nc.vector.tensor_tensor(X[:, bass.ds(k * 4 + t, 1), :], pb[:, t, 0:D].unsqueeze(1),
                                                    X[:, bass.ds(k * 4 + t, 1), :], ALU.add).then_inc(x1_ready, 1)
                            dve.wait_ge(x1_ready, k * 4 + t + 1)
                            apart(dve)
                            nc.vector.bn_stats(st[:, t, :], X[:, bass.ds(k * 4 + t, 1), :].rearrange("p a n -> p (a n)")).then_inc(st_ready, 1)
                            dve.wait_ge(st_ready, k * 4 + t + 1)
                            apart(dve)
                            nc.vector.bn_aggr(mv[:, t, :], st[:, t, :]).then_inc(mv_ready, 1)
                        for t in range(4):
                            dve.wait_ge(rs_ready, k * 4 + t + 1)
                            if t == 0:
                                dve.wait_ge(tr_done, k * 2)
                            nc.vector.tensor_scalar(xnb[:, t, :].unsqueeze(1), X[:, bass.ds(k * 4 + t, 1), :], mv[:, t, 0:1],
                                                    rs[:, t:t + 1], ALU.subtract, ALU.mult).then_inc(xn_done, 1)
                        for c in range(DC):
                            dve.wait_ge(tr_hi, k * 2 + c + 1)
                            nc.vector.tensor_tensor(bl[:, c, :], pb[:, 4 + c, :], bh[:, c, :].bitcast(f32),
                                                    ALU.subtract).then_inc(tr_lo, 1)

                    over_blocks(dve, step)

                @block.gpsimd
                def _(pool):
                    def step(k, first):
                        for t in range(4):
                            pool.wait_ge(mv_ready, k * 4 + t + 1)
                            if t == 0:
                                pool.wait_ge(xn_done, k * 4)
                            apart(pool)
                            nc.gpsimd.tensor_scalar(ve[:, t:t + 1], mv[:, t, 1:2], EPS, None, ALU.add).then_inc(ve_ready, 1)
                            pool.wait_ge(ve_ready, k * 4 + t + 1)
                            nc.gpsimd.tensor_tensor(rs[:, t:t + 1], ve[:, t:t + 1], minus_half[:, 0:1], ALU.pow).then_inc(rs_ready, 1)

                    over_blocks(pool, step)

                @block.tensor
                def _(pe):
                    def project(k, part):
                        if part == 0:
                            pe.wait_ge(tr_lo, k * 2 + 2)
                        for m in range(4) if part == 0 else (4, 5):
                            if m >= 2:
                                pe.wait_ge(p_evac, k * 6 + m - 1)
                            o = pb[:, 6 + m % 2, :]
                            if m < 4:
                                w, co = m // 2, m % 2
                                last = split_mm(o, [((AWh[:, w, ci, co * P:co * P + P], AWl[:, w, ci, co * P:co * P + P]),
                                                     (bh[:, ci, :], bl[:, ci, :])) for ci in range(DC)])
                            else:
                                for h in range(2):
                                    ts = slice(P * (2 * (m - 4) + h), P * (2 * (m - 4) + h) + P)
                                    last = split_mm(o[:, D * h:D * h + D], [((bh[:, ci, ts], bl[:, ci, ts]),
                                                                            (AWh[:, 2, ci, :], AWl[:, 2, ci, :])) for ci in range(DC)])
                            last.then_inc(p_done, 1)

                    def step(k, first):
                        if not first:
                            project(k - 1, 0)
                        pe.wait_ge(o_lo, k * 2 + 2)
                        for t in range(4):
                            if not first:
                                pe.wait_ge(x1_ready, k * 4 + t - 3)
                            ts = slice(P * t, P * t + P)
                            split_mm(pb[:, t, 0:D], [((oh[:, c, ts], ol[:, c, ts]), (XWOh[:, c, :], XWOl[:, c, :])) for c in range(DC)],
                                     stop=False)
                            nc.tensor.matmul(pb[:, t, 0:D], ones_row[:], bias_rows[:, 0, :], start=False, stop=True).then_inc(y_done, 1)
                        if not first:
                            project(k - 1, 1)
                        for c in range(DC):
                            if not first:
                                pe.wait_ge(tr_lo, k * 2 + c - 1)
                            for t in range(4):
                                pe.wait_ge(xn_done, k * 4 + t + 1)
                                last = nc.tensor.transpose(pb[:, 4 + c, P * t:P * t + P], xnb[:, t, c * P:c * P + P], ident[:])
                            last.then_inc(tr_done, 1)

                    over_blocks(pe, step)
                    project(NB - 1, 0)
                    project(NB - 1, 1)

        fin = ExitStack()
        with fin:
            def sf(name, shape, dt=f32):
                return sb(name, shape, dt, fin)

            KB = [sf(f"KB{k}", [P, DC, G, 8, T]) for k in range(2)]
            QS = [sf(f"QS{k}", [P, DC, P]) for k in range(2)]
            VM = [sf(f"VM{k}", [P, G, D]) for k in range(2)]
            logit, shifted, expo, prob = (sf(n, [P, H, T]) for n in ("logit", "shifted", "expo", "prob"))
            probT = sf("probT", [P, H, T])
            nmax, psum_, prec = (sf(n, [P, H]) for n in ("nmax", "psum_", "prec"))
            even2, both2 = sf("even2", [P, DC * G, T]), sf("both2", [P, DC * G, T])
            o2h, o2l = sf("o2h", [P, DC, P], f32r), sf("o2l", [P, DC, P], f32r)
            st2, mv2, ve2, rs2 = sf("st2", [P, 6]), sf("mv2", [P, 2]), sf("ve2", [P, 1]), sf("rs2", [P, 1])
            xn2 = sf("xn2", [P, D])
            gh, gl = sf("gh", [P, DC, P], f32r), sf("gl", [P, DC, P], f32r)
            th, half, hid = sf("th", [P, 2, HID]), sf("half", [P, 2, HID]), sf("hid", [P, 2, HID])
            HTh = [sf(f"HTh{k}", [P, 2, DC, P], f32r) for k in range(2)]
            HTl = [sf(f"HTl{k}", [P, 2, DC, P], f32r) for k in range(2)]
            lg, gexp, gprob, top8, hot0, hot = (sf(n, [P, E]) for n in ("lg", "gexp", "gprob", "top8", "hot0", "hot"))
            gneg, gsum, grec, idf, cols = sf("gneg", [P, 1]), sf("gsum", [P, 1]), sf("grec", [P, 1]), sf("idf", [P, E]), sf("cols", [P, E])
            idx = sf("idx", [P, E], mybir.dt.uint32)
            cols_i = sf("cols_i", [P, E], mybir.dt.int32)
            gw = [sf(f"gw{k}", [P, E]) for k in range(2)]

            names = ("staged", "kb_ready", "s_done", "logit_ready", "nmax_ready", "shift_ready", "exp_done", "psum_ready",
                     "prec_ready", "prob_ready", "probT_ready", "pv_done", "even_ready", "both_ready", "o_hi", "o_lo",
                     "j_done", "x2_ready", "st_ready", "mv_ready", "ve_ready", "rs_ready", "xn_ready", "kt_done", "g_hi",
                     "g_lo", "lg_done", "l_done", "lg_read", "gneg_ready", "gexp_done", "th_done", "half_ready",
                     "hid_ready", "gate_chain", "gw_ready", "m_done", "ht_hi", "ht_lo", "ex_done", "acc_chain", "stored",
                     "vm_zero", "cols_ready")
            F = {n: sem("f_" + n, fin) for n in names}
            psS2, psO2, psJ, psG = pb[:, 0, :], pb[:, 1, :], pb[:, 2, :], pb[:, 3, :]
            LINKS = 8
            ACC = 9

            def pipeline(eng, step):
                for s in (-1, 0, 1):
                    step(s, s % 2)
                with eng.Fori(1, (NT - 2) // 2) as m:
                    for par in range(2):
                        step(m * 2 + par, par)
                for s in range(NT - 2, NT + 1):
                    step(s, s % 2)

            def attends(s):
                return not isinstance(s, int) or s + 1 < NT

            def prepares(s):
                return not isinstance(s, int) or s + 2 < NT

            def hides(s):
                return not isinstance(s, int) or 0 <= s < NT

            def expands(s):
                return not isinstance(s, int) or s >= 1

            def wait(eng, name, value):
                if not isinstance(value, int) or value > 0:
                    eng.wait_ge(F[name], value)

            with nc.Block() as block:

                @block.sync
                def _(sp):
                    out_v = out.rearrange("b t d -> (b t) d").rearrange("(n p) d -> n p d", p=P)

                    with sp.Fori(0, NT) as t:
                        sp.wait_ge(F["acc_chain"], t * ACC + ACC)
                        sp.dma_start(out_v[bass.ds(t, 1)].rearrange("a p n -> p a n"), X[:, bass.ds(t, 1), :]).then_inc(F["stored"], 16)
                    sp.wait_ge(F["stored"], 16 * NT)

                @block.gpsimd
                def _(pool):
                    for k in range(2):
                        last = nc.gpsimd.memset(VM[k][:], 0.0)
                    last.then_inc(F["vm_zero"], 1)
                    nc.gpsimd.iota(cols_i[:], pattern=[[1, E]], base=0, channel_multiplier=0).then_inc(F["cols_ready"], 1)
                    pool.wait_ge(F["cols_ready"], 1)
                    nc.gpsimd.tensor_copy(cols[:], cols_i[:]).then_inc(F["cols_ready"], 1)

                    def keys(t, k, c):
                        src = KTm[:, c, bass.ds(t * P, P)].rearrange("p (b q) -> p b q", b=G).unsqueeze(2).broadcast_to([P, G, 8, T])
                        msk = head_mask[:].unsqueeze(1).unsqueeze(3).broadcast_to([P, G, 8, T])
                        nc.gpsimd.tensor_tensor(KB[k][:, c], src, msk, ALU.mult).then_inc(F["kb_ready"], 1)

                    for c in range(DC):
                        keys(0, 0, c)

                    def step(s, par):
                        u = s + 1
                        if prepares(s):
                            wait(pool, "s_done", u)
                            keys(s + 2, par, 0)
                        if attends(s):
                            wait(pool, "prec_ready", u + 1)
                            wait(pool, "probT_ready", u)
                            nc.gpsimd.tensor_tensor(prob[:], expo[:], prec[:].unsqueeze(2).broadcast_to([P, H, T]),
                                                    ALU.mult).then_inc(F["prob_ready"], 1)
                        if prepares(s):
                            keys(s + 2, par, 1)
                        if attends(s):
                            wait(pool, "mv_ready", u + 1)
                            wait(pool, "xn_ready", u)
                            apart(pool)
                            nc.gpsimd.tensor_scalar(ve2[:], mv2[:, 1:2], EPS, None, ALU.add).then_inc(F["ve_ready"], 1)
                            wait(pool, "ve_ready", u + 1)
                            nc.gpsimd.tensor_tensor(rs2[:], ve2[:], minus_half[:, 0:1], ALU.pow).then_inc(F["rs_ready"], 1)

                    pipeline(pool, step)

                @block.scalar
                def _(act):
                    def stage(t, k):
                        wait(act, "s_done", t - 1)
                        wait(act, "pv_done", t - 1)
                        nc.scalar.activation(QS[k][:], QT[:, :, bass.ds(t * P, P)], ACT.Copy)
                        for b in range(G):
                            r = slice(T * b, T * b + T)
                            last = nc.scalar.activation(VM[k][r, b:b + 1, :], V[r, bass.ds(t, 1), :], ACT.Copy)
                        last.then_inc(F["staged"], 1)

                    act.wait_ge(F["vm_zero"], 1)
                    stage(0, 0)

                    def step(s, par):
                        u = s + 1
                        if hides(s):
                            wait(act, "kt_done", s + 1)
                            wait(act, "l_done", s * 2)
                            nc.scalar.activation(gh[:], psG[:, 0:D].rearrange("p (c t) -> p c t", c=DC), ACT.Copy).then_inc(F["g_hi"], 1)
                        if attends(s):
                            wait(act, "shift_ready", u + 1)
                            wait(act, "prob_ready", u)
                            nc.scalar.activation(expo[:], shifted[:], ACT.Exp).then_inc(F["exp_done"], 1)
                        if hides(s):
                            wait(act, "l_done", s * 2 + 1)
                            nc.scalar.activation(th[:, 0, :], pb[:, 4, 0:HID], ACT.Tanh, scale=0.5).then_inc(F["th_done"], 1)
                            wait(act, "gneg_ready", s + 1)
                            nc.scalar.activation(gexp[:], lg[:], ACT.Exp, bias=gneg[:], accum_out=gsum[:]).then_inc(F["gexp_done"], 1)
                            wait(act, "l_done", s * 2 + 2)
                            nc.scalar.activation(th[:, 1, :], pb[:, 5, 0:HID], ACT.Tanh, scale=0.5).then_inc(F["th_done"], 1)
                        if prepares(s):
                            stage(s + 2, par)
                        if attends(s):
                            wait(act, "both_ready", u + 1)
                            wait(act, "j_done", u)
                            for c in range(DC):
                                last = nc.scalar.activation(o2h[:, c, :].rearrange("p (b q) -> p b q", b=G), both2[:, G * c:G * c + G, :],
                                                            ACT.Identity, bias=bcol[:, 3, c:c + 1])
                            last.then_inc(F["o_hi"], 1)
                        if hides(s):
                            wait(act, "m_done", s + 1)
                            if not isinstance(s, int) or s >= 2:
                                wait(act, "ex_done", (s - 1) * 5)
                            nc.scalar.activation(HTh[par][:], psG.rearrange("p (a c t) -> p a c t", a=2, c=DC), ACT.Copy).then_inc(F["ht_hi"], 1)

                    pipeline(act, step)

                @block.vector
                def _(dve):
                    dve.wait_ge(F["cols_ready"], 2)

                    def accumulate(t, par, units):
                        xt = X[:, bass.ds(t, 1), :]
                        for m in units:
                            wait(dve, "ex_done", t * 5 + m + 1)
                            bank = 6 + (m + par) % 2
                            for h in range(1 if m == 0 else 2):
                                k = 0 if m == 0 else 2 * m - 1 + h
                                wait(dve, "acc_chain", t * ACC + k)
                                ps = pb[:, bank, D * h:D * h + D].unsqueeze(1)
                                if m == 0:
                                    wait(dve, "x2_ready", t + 1)
                                    last = nc.vector.tensor_tensor(xt, ps, xt, ALU.add)
                                else:
                                    e = 2 * (m - 1) + h
                                    if k == 1:
                                        wait(dve, "gw_ready", t + 1)
                                    last = nc.vector.scalar_tensor_tensor(xt, ps, gw[par][:, e:e + 1], xt, ALU.mult, ALU.add)
                                last.then_inc(F["acc_chain"], 1)

                    def step(s, par):
                        u, po = s + 1, 1 - par
                        if attends(s):
                            wait(dve, "s_done", u + 1)
                            nc.vector.tensor_tensor(logit[:], psS2.rearrange("p (h k) -> p h k", h=H),
                                                    decay[:].unsqueeze(1).broadcast_to([P, H, T]), ALU.add).then_inc(F["logit_ready"], 1)
                            wait(dve, "logit_ready", u + 1)
                            nc.vector.tensor_reduce(nmax[:], logit[:], AX.X, ALU.max, negate=True).then_inc(F["nmax_ready"], 1)
                            wait(dve, "nmax_ready", u + 1)
                            wait(dve, "exp_done", u)
                            nc.vector.tensor_tensor(shifted[:], logit[:], nmax[:].unsqueeze(2).broadcast_to([P, H, T]),
                                                    ALU.add).then_inc(F["shift_ready"], 1)
                        if hides(s):
                            wait(dve, "g_hi", s + 1)
                            nc.vector.tensor_tensor(gl[:], psG[:, 0:D].rearrange("p (c t) -> p c t", c=DC), gh[:].bitcast(f32),
                                                    ALU.subtract).then_inc(F["g_lo"], 1)
                        if expands(s):
                            accumulate(s - 1, po, (0,))
                        if attends(s):
                            wait(dve, "exp_done", u + 1)
                            nc.vector.tensor_reduce(psum_[:], expo[:], AX.X, ALU.add).then_inc(F["psum_ready"], 1)
                            wait(dve, "psum_ready", u + 1)
                            nc.vector.reciprocal(prec[:], psum_[:]).then_inc(F["prec_ready"], 1)
                        if expands(s):
                            accumulate(s - 1, po, (1,))
                        if attends(s):
                            wait(dve, "prob_ready", u + 1)
                            wait(dve, "pv_done", u)
                            nc.vector.transpose(probT[:].rearrange("p h q -> p (h q)"), prob[:].rearrange("p h k -> p (h k)")).then_inc(F["probT_ready"], 1)
                        if expands(s):
                            accumulate(s - 1, po, (2,))
                        if hides(s):
                            wait(dve, "lg_done", s + 1)
                            wait(dve, "gexp_done", s)
                            nc.vector.tensor_tensor(lg[:], psG[:, 0:E], gate_b[:], ALU.add).then_inc(F["lg_read"], 1)
                            wait(dve, "lg_read", s + 1)
                            nc.vector.tensor_reduce(gneg[:], lg[:], AX.X, ALU.max, negate=True).then_inc(F["gneg_ready"], 1)
                            for a in range(2):
                                wait(dve, "th_done", s * 2 + a + 1)
                                nc.vector.scalar_tensor_tensor(half[:, a, :], th[:, a, :], 1.0, pb[:, 4 + a, 0:HID], ALU.add, ALU.mult).then_inc(F["half_ready"], 1)
                                wait(dve, "half_ready", s * 2 + a + 1)
                                if a == 0:
                                    wait(dve, "m_done", s)
                                nc.vector.scalar_tensor_tensor(hid[:, a, :], half[:, a, :], 0.5, pb[:, 4 + a, HID:2 * HID],
                                                               ALU.mult, ALU.mult).then_inc(F["hid_ready"], 1)
                            wait(dve, "gexp_done", s + 1)
                            chain = [
                                lambda: nc.vector.reciprocal(grec[:], gsum[:]),
                                lambda: nc.vector.tensor_scalar(gprob[:], gexp[:], grec[:], None, ALU.mult),
                                lambda: nc.vector.max(top8[:], gprob[:]),
                                lambda: nc.vector.max_index(idx[:], top8[:], gprob[:]),
                                lambda: nc.vector.tensor_copy(idf[:], idx[:]),
                                lambda: nc.vector.tensor_scalar(hot0[:], cols[:], idf[:, 0:1], None, ALU.is_equal),
                                lambda: nc.vector.scalar_tensor_tensor(hot[:], cols[:], idf[:, 1:2], hot0[:], ALU.is_equal, ALU.add),
                            ]
                            for k, op in enumerate(chain):
                                if k in (2, 3):
                                    apart(dve)
                                op().then_inc(F["gate_chain"], 1)
                                wait(dve, "gate_chain", s * len(chain) + k + 1)
                            nc.vector.tensor_tensor(gw[par][:], hot[:], gprob[:], ALU.mult).then_inc(F["gw_ready"], 1)
                        if attends(s):
                            wait(dve, "pv_done", u + 1)
                            o = psO2.rearrange("p (cb e q) -> p cb e q", e=2, q=T)
                            nc.vector.tensor_scalar(even2[:], o[:, :, 0, :], pair_mask[:, 0:1], None, ALU.mult).then_inc(F["even_ready"], 1)
                            wait(dve, "even_ready", u + 1)
                            wait(dve, "o_hi", u)
                            nc.vector.scalar_tensor_tensor(both2[:], o[:, :, 1, :], pair_mask[:, 1:2], even2[:], ALU.mult, ALU.add).then_inc(F["both_ready"], 1)
                        if expands(s):
                            accumulate(s - 1, po, (3,))
                        if attends(s):
                            wait(dve, "o_hi", u + 1)
                            for c in range(DC):
                                last = nc.vector.scalar_tensor_tensor(o2l[:, c, :].rearrange("p (b q) -> p b q", b=G), both2[:, G * c:G * c + G, :],
                                                                      bcol[:, 3, c:c + 1], o2h[:, c, :].bitcast(f32).rearrange("p (b q) -> p b q", b=G),
                                                                      ALU.add, ALU.subtract)
                            last.then_inc(F["o_lo"], 1)
                        if hides(s):
                            wait(dve, "ht_hi", s + 1)
                            nc.vector.tensor_tensor(HTl[par][:].rearrange("p a c t -> p (a c t)"), psG, HTh[par][:].bitcast(f32).rearrange("p a c t -> p (a c t)"),
                                                    ALU.subtract).then_inc(F["ht_lo"], 1)
                        if attends(s):
                            wait(dve, "j_done", u + 1)
                            xu = X[:, bass.ds(u, 1), :]
                            nc.vector.tensor_tensor(xu, psJ[:, 0:D].unsqueeze(1), xu, ALU.add).then_inc(F["x2_ready"], 1)
                            wait(dve, "x2_ready", u + 1)
                            apart(dve)
                            nc.vector.bn_stats(st2[:], xu.rearrange("p a n -> p (a n)")).then_inc(F["st_ready"], 1)
                            wait(dve, "st_ready", u + 1)
                            apart(dve)
                            nc.vector.bn_aggr(mv2[:], st2[:]).then_inc(F["mv_ready"], 1)
                        if expands(s):
                            accumulate(s - 1, po, (4,))
                        if attends(s):
                            wait(dve, "rs_ready", u + 1)
                            wait(dve, "kt_done", u)
                            nc.vector.tensor_scalar(xn2[:].unsqueeze(1), xu, mv2[:, 0:1], rs2[:], ALU.subtract, ALU.mult).then_inc(F["xn_ready"], 1)

                    pipeline(dve, step)

                @block.tensor
                def _(pe):
                    def experts(t, par, units):
                        wait(pe, "ht_lo", t + 1)
                        for m in units:
                            freed = t * ACC + (-2, 0, 1, 3, 5)[m]
                            if not isinstance(t, int) or freed > 0:
                                wait(pe, "acc_chain", freed)
                            bank = 6 + (m + par) % 2
                            if m == 0:
                                last = split_mm(pb[:, bank, 0:D], [((HTh[par][:, 0, c], HTl[par][:, 0, c]), (WSh[:, c], WSl[:, c])) for c in range(DC)])
                            else:
                                last = split_mm(pb[:, bank, :].rearrange("p (e n) -> p e n", e=2),
                                                [((HTh[par][:, 1, c], HTl[par][:, 1, c]),
                                                  (W2h[:, 4 * (m - 1) + c:4 * m:2, :], W2l[:, 4 * (m - 1) + c:4 * m:2, :])) for c in range(DC)])
                            last.then_inc(F["ex_done"], 1)

                    def step(s, par):
                        u, po = s + 1, 1 - par
                        if attends(s):
                            wait(pe, "kb_ready", u * 2 + 2)
                            wait(pe, "staged", u + 1)
                            wait(pe, "logit_ready", u)
                            for c in range(DC):
                                for b in range(G):
                                    last = nc.tensor.matmul(psS2[T * b:T * b + T, 256 * c:256 * c + 256], QS[po][:, c, T * b:T * b + T],
                                                            KB[po][:, c, b].rearrange("p h q -> p (h q)"), start=c == 0, stop=c == DC - 1,
                                                            skip_group_check=True)
                            last.then_inc(F["s_done"], 1)
                        if hides(s):
                            wait(pe, "xn_ready", s + 1)
                            wait(pe, "ht_lo", s)
                            for c in range(DC):
                                last = nc.tensor.transpose(psG[:, P * c:P * c + P], xn2[:, P * c:P * c + P], ident[:])
                            last.then_inc(F["kt_done"], 1)
                        if expands(s):
                            experts(s - 1, po, (0, 1, 2))
                        if hides(s):
                            wait(pe, "g_lo", s + 1)
                            split_mm(psG[:, 0:E], [((gh[:, c], gl[:, c]), (WGh[:, c], WGl[:, c])) for c in range(DC)]).then_inc(F["lg_done"], 1)
                            wait(pe, "hid_ready", s * 2)
                            for a in range(2):
                                split_mm(pb[:, 4 + a, :], [((gh[:, c], gl[:, c]), (WIh[:, c, a, :], WIl[:, c, a, :])) for c in range(DC)]).then_inc(F["l_done"], 1)
                        if attends(s):
                            wait(pe, "probT_ready", u + 1)
                            wait(pe, "both_ready", u)
                            for b in range(G):
                                for c in range(DC):
                                    o = (c * G + b) * 64
                                    for jj in range(4):
                                        h0 = c * 8 + 2 * jj
                                        last = nc.tensor.matmul(psO2[32 * jj:32 * jj + 32, o:o + 64], VM[po][:, b, c * P + 32 * jj:c * P + 32 * jj + 32],
                                                                probT[:, h0:h0 + 2, :].rearrange("p h q -> p (h q)"), start=(b, c) == (0, 0),
                                                                stop=(b, c) == (G - 1, DC - 1), skip_group_check=True)
                            last.then_inc(F["pv_done"], 1)
                        if expands(s):
                            experts(s - 1, po, (3,))
                        if hides(s):
                            wait(pe, "hid_ready", s * 2 + 2)
                            wait(pe, "lg_read", s + 1)
                            for a in range(2):
                                for c in range(DC):
                                    o = (a * DC + c) * P
                                    last = nc.tensor.transpose(psG[:, o:o + P], hid[:, a, P * c:P * c + P], ident[:])
                            last.then_inc(F["m_done"], 1)
                        if attends(s):
                            wait(pe, "o_lo", u + 1)
                            wait(pe, "x2_ready", u)
                            split_mm(psJ[:, 0:D], [((o2h[:, c], o2l[:, c]), (AWh[:, 3, c, :], AWl[:, 3, c, :])) for c in range(DC)], stop=False)
                            nc.tensor.matmul(psJ[:, 0:D], ones_row[:], bias_rows[:, 1, :], start=False, stop=True).then_inc(F["j_done"], 1)
                        if expands(s):
                            experts(s - 1, po, (4,))

                    pipeline(pe, step)


_INS = ['x', 'ctx_768', 'L0_xattn_Wq', 'L0_xattn_bq', 'L0_xattn_Wk', 'L0_xattn_bk', 'L0_xattn_Wv', 'L0_xattn_bv',
        'L0_xattn_Wo', 'L0_xattn_bo', 'L0_attn_Wq', 'L0_attn_bq', 'L0_attn_Wk', 'L0_attn_bk', 'L0_attn_Wv',
        'L0_attn_bv', 'L0_attn_Wo', 'L0_attn_bo', 'L0_ffn_w_shared_in', 'L0_ffn_w_shared_out', 'L0_ffn_w1_shared',
        'L0_ffn_w2', 'L0_ffn_w_gate', 'L0_ffn_gate_bias']
_OUTS = [((64, 32, 256), 'float32')]


def kernel(**inputs):
    import numpy as _np
    import concourse.bacc as _bacc
    from concourse import mybir as _mybir
    from concourse.bass_utils import run_bass_kernel_spmd as _run

    nc = _bacc.Bacc("TRN2", target_bir_lowering=False, num_devices=1)
    arrays, args = {}, []
    for name in _INS:
        a = _np.ascontiguousarray(inputs[name])
        arrays[f"in_{name}_dram"] = a
        args.append(nc.dram_tensor(f"in_{name}_dram", a.shape, _mybir.dt.from_np(a.dtype), kind="ExternalInput").ap())
    for i, (shape, dtype) in enumerate(_OUTS):
        dt = _mybir.dt.from_np(_np.dtype(dtype))
        args.append(nc.dram_tensor(f"out_{i}_dram", shape, dt, kind="ExternalOutput").ap())
    perceiver_kernel(nc, *args)
    r = _run(nc, [arrays], core_ids=[0])
    got = tuple(r.results[0][f"out_{i}_dram"] for i in range(len(_OUTS)))
    return got[0]
```

```python
import concourse.bass as bass
from concourse import mybir
from contextlib import ExitStack

f32 = mybir.dt.float32
f32r = mybir.dt.float32r
ALU = mybir.AluOpType
ACT = mybir.ActivationFunctionType
AX = mybir.AxisListType

B, T, D = 64, 32, 256
S, C = 257, 192
H, HD = 16, 16
P = 128
TOK = B * T
NT = TOK // P
G = P // T
NG = B // G
HG = P // T
NHG = H // HG
DC = D // P
KT = 2
E, HID = 8, 256
SCALE = HD ** -0.5
CLAMP = 10000.0
EPS = 1e-5
LAST = S - 1
SP_ = S + 1
MASKED = -3.0e38


def perceiver_kernel(nc, x, ctx, xwq, xbq, xwk, xbk, xwv, xbv, xwo, xbo, awq, abq, awk, abk, awv, abv,
                     awo, abo, w_in, w_out, w1, w2, w_gate, gate_bias, out):
    stack = ExitStack()
    with stack:
        def sb(name, shape, dt=f32, on=stack):
            return on.enter_context(nc.sbuf_tensor(name, shape, dt))

        def sem(name, on=stack):
            return on.enter_context(nc.semaphore(name))

        pb = stack.enter_context(nc.psum_tensor("pb", [P, 8, 512], f32))
        ident = sb("ident", [P, P])
        head_mask = sb("head_mask", [P, 8])
        pair_mask = sb("pair_mask", [P, 2])
        X = sb("X", [P, NT, D])
        OT = sb("OT", [P, NT, DC, P])
        W2h = sb("W2h", [P, NG, D], f32r)
        W2l = sb("W2l", [P, NG, D], f32r)
        mean_var = sb("mean_var", [P, NT, 2])
        bnst = sb("bnst", [P, NT, 6])
        var_eps = sb("var_eps", [P, NT])
        rstd = sb("rstd", [P, NT])
        minus_half = sb("minus_half", [P, NT])
        QT = sb("QT", [P, DC, TOK])
        bcol = sb("bcol", [P, 4, DC])
        gate_b = sb("gate_b", [P, E])
        aw_raw = QT[:, 0, :].rearrange("p (k c n) -> p k c n", k=4, c=DC)
        wi_raw = QT[:, 1, :].rearrange("p (c k n) -> p c k n", c=DC, k=2)
        xwo_raw = sb("xwo_raw", [P, DC, D])
        brow_raw = sb("brow_raw", [33, 2, D])
        raw_in = sem("raw_in")
        RAW_LOADS = 16

        def apart(eng):
            eng.nop(nofuse=True)


        cross = ExitStack()
        with cross:
            def sc(name, shape, dt=f32):
                return sb(name, shape, dt, cross)

            KVh = sc("KVh", [P, 2, 2, D], f32r)
            KVl = sc("KVl", [P, 2, 2, D], f32r)
            QTh = sc("QTh", [P, DC, TOK], f32r)
            QTl = sc("QTl", [P, DC, TOK], f32r)
            KL = sc("KL", [P, B, DC, 2], f32r)
            VL = sc("VL", [G, NG, D])
            bk = sc("bk", [P, DC])
            stacked_id = sc("stacked_id", [P, T])
            head_rows = sc("head_rows", [P, 2, P], f32r)

            CX = [sc(f"CX{k}", [P, KT, C]) for k in range(4)]
            ctx_in = [sem(f"ctx_in{k}", cross) for k in range(4)]
            ctx_v = ctx[:, 0:KT * P, :].rearrange("b (p t) c -> b p t c", t=KT)

            pro = ExitStack()
            with pro:
                def sp0(name, shape, dt=f32):
                    return sb(name, shape, dt, pro)

                kvraw = sp0("kvraw", [P, 2, 2, D])
                wqraw = sp0("wqraw", [P, DC, D])
                WQh = sp0("WQh", [P, DC, D], f32r)
                WQl = sp0("WQl", [P, DC, D], f32r)
                bq = sp0("bq", [P, DC])
                xTh = sp0("xTh", [P, DC, TOK], f32r)
                xTl = sp0("xTl", [P, DC, TOK], f32r)
                bq4 = sp0("bq_scaled", [P, DC])
                shift = sp0("shift", [P, NT])
                ctxl = sp0("ctxl", [B, C])
                CL = sp0("CL", [P, 3, B], f32r)
                VLa = sp0("VLa", [B, D])
                ones = sp0("ones", [P, P])
                head_rows_raw = sp0("head_rows_raw", [P, 2, P])
                hmt = sp0("hmt", [P, 8])
                hrt = sp0("hrt", [P, 4, 16])
                xn = OT[:].rearrange("p t c n -> p t (c n)")

                x_in = [sem(f"x_in{b}", pro) for b in range(4)]
                wq_in, kv_in, bias_in, cl_in = (sem(n, pro) for n in ("wq_in", "kv_in", "bias_in", "cl_in"))
                vl_in, consts, const_step = (sem(n, pro) for n in ("vl_in", "consts", "const_step"))
                stats, aggr, eps_added, rstd_ready, shift_step, xn_dve, xn_act, bq_scaled = (
                    sem(n, pro) for n in ("stats", "aggr", "eps_added", "rstd_ready", "shift_step", "xn_dve", "xn_act", "bq_scaled"))
                xt_done, xt_hi, xt_lo, q_done, q_hi, q_lo = (
                    sem(n, pro) for n in ("xt_done", "xt_hi", "xt_lo", "q_done", "q_hi", "q_lo"))
                wq_hi, wq_lo, kv_hi, kv_lo = (sem(n, pro) for n in ("wq_hi", "wq_lo", "kv_hi", "kv_lo"))
                cl_t, cl_hi, cl_lo, left_k, left_v, kl_hi, kl_lo, vl_out = (
                    sem(n, pro) for n in ("cl_t", "cl_hi", "cl_lo", "left_k", "left_v", "kl_hi", "kl_lo", "vl_out"))

                x_v = x.rearrange("b t d -> (b t) d").rearrange("(n p) d -> p n d", p=P)
                with nc.Block() as block:

                    @block.sync
                    def _(sp):
                        sp.dma_start(X[:, 0:4, :], x_v[:, 0:4, :]).then_inc(x_in[0], 16)
                        sp.dma_start(wqraw[:], xwq.rearrange("(c p) n -> p c n", p=P)).then_inc(wq_in, 16)
                        for b in range(1, 4):
                            sp.dma_start(X[:, 4 * b:4 * b + 4, :], x_v[:, 4 * b:4 * b + 4, :]).then_inc(x_in[b], 16)
                        for k, w in enumerate((xwk, xwv)):
                            sp.dma_start(kvraw[:, k, 0, :], w[0:P, :]).then_inc(kv_in, 16)
                            sp.dma_start(kvraw[0:64, k, 1, :], w[P:C, :]).then_inc(kv_in, 16)
                            sp.dma_start(kvraw[64:P, k, 1, :], w[P:C, :]).then_inc(kv_in, 16)
                        sp.dma_start(ctxl[:], ctx[:, LAST, :]).then_inc(cl_in, 16)
                        for k in range(4):
                            sp.dma_start(CX[k][:], ctx_v[k]).then_inc(ctx_in[k], 16)
                        sp.wait_ge(vl_out, 1)
                        for r in range(G):
                            sp.dma_start(VL[r:r + 1, :, :], VLa[r:B:G, :]).then_inc(vl_in, 16)
                        sp.wait_ge(vl_in, 16 * G)

                    @block.gpsimd
                    def _(pool):
                        with nc.allow_non_contiguous_dma(reason="biases, one element per partition"):
                            pool.dma_start(bq[:], xbq.rearrange("(c p) -> p c", p=P)).then_inc(bias_in, 16)
                            pool.dma_start(bk[:], xbk.rearrange("(c p) -> p c", p=P)).then_inc(bias_in, 16)
                        nc.gpsimd.memset(ident[:], 0.0)
                        nc.gpsimd.memset(ones[:], 1.0)
                        nc.gpsimd.memset(head_rows_raw[:], 0.0)
                        nc.gpsimd.memset(minus_half[:], -0.5).then_inc(const_step, 1)
                        pool.wait_ge(const_step, 1)
                        nc.gpsimd.affine_select(out=ident[:], in_=ident[:], compare_op=ALU.not_equal, fill=1.0,
                                                base=0, pattern=[[-1, P]], channel_multiplier=1)
                        nc.gpsimd.affine_select(out=hmt[:], in_=ones[:, 0:8], compare_op=ALU.is_ge, fill=0.0,
                                                base=0, pattern=[[-HD, 8]], channel_multiplier=1)
                        nc.gpsimd.affine_select(out=hrt[:], in_=ones[:, 0:64].rearrange("p (h d) -> p h d", d=16),
                                                compare_op=ALU.is_ge, fill=0.0, base=0,
                                                pattern=[[-T, 4], [0, 16]], channel_multiplier=1).then_inc(const_step, 1)
                        pool.wait_ge(const_step, 2)
                        nc.gpsimd.affine_select(out=head_mask[:], in_=hmt[:], compare_op=ALU.is_ge, fill=0.0,
                                                base=HD - 1, pattern=[[HD, 8]], channel_multiplier=-1)
                        for par in range(2):
                            o = head_rows_raw[:, par, 64 * par:64 * par + 64].rearrange("p (h d) -> p h d", d=16)
                            last = nc.gpsimd.affine_select(out=o, in_=hrt[:], compare_op=ALU.is_ge, fill=0.0,
                                                           base=T - 1, pattern=[[T, 4], [0, 16]], channel_multiplier=-1)
                        last.then_inc(consts, 1)
                        for b in range(4):
                            t = slice(4 * b, 4 * b + 4)
                            pool.wait_ge(aggr, b + 1)
                            nc.gpsimd.tensor_scalar(var_eps[:, t], mean_var[:, t, 1], EPS, None, ALU.add).then_inc(eps_added, 1)
                            pool.wait_ge(eps_added, b + 1)
                            nc.gpsimd.tensor_tensor(rstd[:, t], var_eps[:, t], minus_half[:, t], ALU.pow).then_inc(rstd_ready, 1)
                            pool.wait_ge(rstd_ready, b + 1)
                            nc.gpsimd.tensor_tensor(shift[:, t], mean_var[:, t, 0], rstd[:, t], ALU.mult).then_inc(shift_step, 1)
                            pool.wait_ge(shift_step, 2 * b + 1)
                            nc.gpsimd.tensor_scalar(shift[:, t], shift[:, t], -1.0, None, ALU.mult).then_inc(shift_step, 1)

                    @block.scalar
                    def _(act):
                        def normalise(b):
                            act.wait_ge(shift_step, 2 * b + 2)
                            for t in (4 * b + 2, 4 * b + 3):
                                last = nc.scalar.activation(xn[:, t, :], X[:, t, :], ACT.Identity, bias=shift[:, t:t + 1],
                                                            scale=rstd[:, t:t + 1])
                            last.then_inc(xn_act, 1)

                        def split_x(b):
                            for c in range(DC):
                                act.wait_ge(xt_done, 2 * b + c + 1)
                                nc.scalar.activation(xTh[:, c, 512 * b:512 * b + 512], pb[:, 2 * (b % 2) + c, :],
                                                     ACT.Copy).then_inc(xt_hi, 1)

                        def split_q(b):
                            for co in range(DC):
                                act.wait_ge(q_done, 2 * b + co + 1)
                                nc.scalar.activation(QTh[:, co, 512 * b:512 * b + 512], pb[:, 4 + co, :], ACT.Identity,
                                                     bias=bq4[:, co:co + 1]).then_inc(q_hi, 1)

                        act.wait_ge(wq_in, 16)
                        nc.scalar.activation(WQh[:], wqraw[:], ACT.Copy, scale=SCALE).then_inc(wq_hi, 1)
                        normalise(0)
                        normalise(1)
                        split_x(0)
                        normalise(2)
                        split_x(1)
                        act.wait_ge(bq_scaled, 1)
                        split_q(0)
                        normalise(3)
                        split_x(2)
                        split_q(1)
                        act.wait_ge(kv_in, 96)
                        nc.scalar.activation(KVh[:], kvraw[:], ACT.Copy).then_inc(kv_hi, 1)
                        act.wait_ge(cl_t, 1)
                        nc.scalar.activation(CL[:, 0, :], pb[:, 6, 0:B], ACT.Copy)
                        nc.scalar.activation(CL[0:64, 2, :], pb[0:64, 6, B:2 * B], ACT.Copy).then_inc(cl_hi, 1)
                        split_x(3)
                        split_q(2)
                        act.wait_ge(left_v, 1)
                        nc.scalar.activation(VLa[:], pb[0:B, 6, 256:512], ACT.Copy).then_inc(vl_out, 1)
                        act.wait_ge(left_k, 1)
                        for c in range(DC):
                            last = nc.scalar.activation(KL[:, :, c, 0], pb[:, 7, c * B:c * B + B], ACT.Identity,
                                                        bias=bk[:, c:c + 1])
                        last.then_inc(kl_hi, 1)
                        split_q(3)

                    @block.vector
                    def _(dve):
                        def statistics(b):
                            dve.wait_ge(x_in[b], 16)
                            for t in range(4 * b, 4 * b + 4):
                                last = nc.vector.bn_stats(bnst[:, t, :], X[:, t, :])
                            last.then_inc(stats, 1)
                            dve.wait_ge(stats, b + 1)
                            for t in range(4 * b, 4 * b + 4):
                                last = nc.vector.bn_aggr(mean_var[:, t, :], bnst[:, t, :])
                            last.then_inc(aggr, 1)

                        def normalise(b):
                            dve.wait_ge(rstd_ready, b + 1)
                            for t in (4 * b, 4 * b + 1):
                                last = nc.vector.tensor_scalar(xn[:, t, :], X[:, t, :], mean_var[:, t, 0:1],
                                                               rstd[:, t:t + 1], ALU.subtract, ALU.mult)
                            last.then_inc(xn_dve, 1)

                        def split_x(b):
                            for c in range(DC):
                                dve.wait_ge(xt_hi, 2 * b + c + 1)
                                nc.vector.tensor_tensor(xTl[:, c, 512 * b:512 * b + 512], pb[:, 2 * (b % 2) + c, :],
                                                        xTh[:, c, 512 * b:512 * b + 512].bitcast(f32),
                                                        ALU.subtract).then_inc(xt_lo, 1)

                        def split_q(b):
                            for co in range(DC):
                                dve.wait_ge(q_hi, 2 * b + co + 1)
                                nc.vector.scalar_tensor_tensor(QTl[:, co, 512 * b:512 * b + 512], pb[:, 4 + co, :], bq4[:, co:co + 1],
                                                               QTh[:, co, 512 * b:512 * b + 512].bitcast(f32),
                                                               ALU.add, ALU.subtract).then_inc(q_lo, 1)

                        nc.vector.memset(KVl[64:P, :, 1, :].bitcast(f32), 0.0)
                        statistics(0)
                        dve.wait_ge(wq_hi, 1)
                        nc.vector.scalar_tensor_tensor(WQl[:], wqraw[:], SCALE, WQh[:].bitcast(f32), ALU.mult, ALU.subtract).then_inc(wq_lo, 1)
                        statistics(1)
                        normalise(0)
                        statistics(2)
                        normalise(1)
                        split_x(0)
                        dve.wait_ge(bias_in, 32)
                        nc.vector.tensor_scalar(bq4[:], bq[:], SCALE, None, ALU.mult).then_inc(bq_scaled, 1)
                        statistics(3)
                        normalise(2)
                        split_x(1)
                        dve.wait_ge(bq_scaled, 1)
                        split_q(0)
                        normalise(3)
                        split_x(2)
                        split_q(1)
                        dve.wait_ge(kv_hi, 1)
                        for k in range(2):
                            nc.vector.tensor_tensor(KVl[:, k, 0, :], kvraw[:, k, 0, :], KVh[:, k, 0, :].bitcast(f32), ALU.subtract)
                            last = nc.vector.tensor_tensor(KVl[0:64, k, 1, :], kvraw[0:64, k, 1, :],
                                                           KVh[0:64, k, 1, :].bitcast(f32), ALU.subtract)
                        last.then_inc(kv_lo, 1)
                        dve.wait_ge(cl_hi, 1)
                        nc.vector.tensor_tensor(CL[:, 1, :], pb[:, 6, 0:B], CL[:, 0, :].bitcast(f32), ALU.subtract)
                        nc.vector.tensor_tensor(CL[64:P, 2, :], pb[0:64, 6, B:2 * B], CL[0:64, 2, :].bitcast(f32),
                                                ALU.subtract).then_inc(cl_lo, 1)
                        split_x(3)
                        split_q(2)
                        dve.wait_ge(kl_hi, 1)
                        for c in range(DC):
                            last = nc.vector.scalar_tensor_tensor(KL[:, :, c, 1], pb[:, 7, c * B:c * B + B], bk[:, c:c + 1],
                                                                  KL[:, :, c, 0].bitcast(f32), ALU.add, ALU.subtract)
                        last.then_inc(kl_lo, 1)
                        dve.wait_ge(consts, 1)
                        nc.vector.tensor_copy(head_rows[:], head_rows_raw[:])
                        nc.vector.tensor_reduce(pair_mask[:], head_mask[:].rearrange("p (j e) -> p e j", e=2), AX.X, ALU.add)
                        nc.vector.tensor_reduce(stacked_id[:], ident[:].rearrange("p (b q) -> p q b", q=T), AX.X, ALU.add)
                        split_q(3)

                    @block.tensor
                    def _(pe):
                        def transpose_x(b):
                            pe.wait_ge(xn_dve, b + 1)
                            pe.wait_ge(xn_act, b + 1)
                            for c in range(DC):
                                if b >= 2:
                                    pe.wait_ge(xt_lo, 2 * (b - 2) + c + 1)
                                for t in range(4):
                                    last = nc.tensor.transpose(pb[:, 2 * (b % 2) + c, P * t:P * t + P],
                                                               xn[:, 4 * b + t, c * P:c * P + P], ident[:])
                                last.then_inc(xt_done, 1)

                        def project(b):
                            pe.wait_ge(xt_lo, 2 * b + 2)
                            for co in range(DC):
                                if b:
                                    pe.wait_ge(q_lo, 2 * b + co - 1)
                                cs = slice(co * P, co * P + P)
                                bs = slice(512 * b, 512 * b + 512)
                                for ci in range(DC):
                                    for m, (w, t) in enumerate(((WQh, xTh), (WQh, xTl), (WQl, xTh))):
                                        last = nc.tensor.matmul(pb[:, 4 + co, :], w[:, ci, cs], t[:, ci, bs],
                                                                start=(ci, m) == (0, 0), stop=(ci, m) == (1, 2))
                                last.then_inc(q_done, 1)

                        pe.wait_ge(consts, 1)
                        transpose_x(0)
                        transpose_x(1)
                        pe.wait_ge(wq_lo, 1)
                        project(0)
                        transpose_x(2)
                        pe.wait_ge(cl_in, 16)
                        nc.tensor.transpose(pb[:, 6, 0:B], ctxl[:, 0:P], ident[0:B, 0:B])
                        nc.tensor.transpose(pb[0:64, 6, B:2 * B], ctxl[:, P:C], ident[0:B, 0:B]).then_inc(cl_t, 1)
                        project(1)
                        transpose_x(3)
                        project(2)
                        pe.wait_ge(kv_lo, 1)
                        pe.wait_ge(cl_lo, 1)
                        passes = ((KVh[:, 1, 0, :], 0), (KVh[:, 1, 0, :], 1), (KVl[:, 1, 0, :], 0),
                                  (KVh[:, 1, 1, :], 2), (KVl[:, 1, 1, :], 2))
                        for m, (w, t) in enumerate(passes):
                            last = nc.tensor.matmul(pb[0:B, 6, 256:512], CL[:, t, :], w, start=m == 0, stop=m == 4)
                        last.then_inc(left_v, 1)
                        for c in range(DC):
                            cs = slice(c * P, c * P + P)
                            passes = ((KVh[:, 0, 0, cs], 0), (KVh[:, 0, 0, cs], 1), (KVl[:, 0, 0, cs], 0),
                                      (KVh[:, 0, 1, cs], 2), (KVl[:, 0, 1, cs], 2))
                            for m, (w, t) in enumerate(passes):
                                last = nc.tensor.matmul(pb[:, 7, c * B:c * B + B], w, CL[:, t, :], start=m == 0, stop=m == 4)
                        last.then_inc(left_k, 1)
                        project(3)

            TR = [sc(f"TR{k}", [P, 3, KT * P], f32r) for k in range(2)]
            KR = [sc(f"KR{k}", [P, DC, 2, SP_], f32r) for k in range(2)]
            VR = [sc(f"VR{k}", [P, KT, D]) for k in range(2)]
            QB = [sc(f"QB{k}", [P, 2, DC, 8, T], f32r) for k in range(2)]
            SC = [sc(f"SC{k}", [P, NHG, S]) for k in range(2)]
            PR = sc("PR", [P, NHG, S])
            PTs = sc("PTs", [P, KT, NHG * P])
            PL = sc("PL", [P, NHG, G])
            PLT = sc("PLT", [G, H // 2, G, 2 * T])
            VLg = sc("VLg", [G, D])
            neg_max = [sc(f"neg_max{k}", [P, NHG]) for k in range(2)]
            sums = sc("sums", [P, NHG, G])
            recip = sc("recip", [P, NHG, G])
            recip_hi, recip_lo = sc("recip_hi", [P, NHG, G], f32r), sc("recip_lo", [P, NHG, G])
            RSTh, RSTl = sc("RSTh", [P, NHG * G, T], f32r), sc("RSTl", [P, NHG * G, T], f32r)
            even_part = sc("even_part", [P, DC * G, T])
            w2raw = sc("w2raw", [P, D])

            names = ("t_done", "t_hi", "t_lo", "k_done", "k_hi", "k_lo", "qk_ready", "v_done", "v_evac", "s_done",
                     "clipped", "neg_max_ready", "exp_done", "pl_copied", "vl_ready", "pt_done", "pt_evac",
                     "plt_done", "plt_evac", "pv_done", "pvl_done", "recip_done", "rst_ready", "rt_done", "even_done",
                     "both_done", "o_free", "recip_split", "rst_lo_ready", "w2_in", "w2_hi", "w2_lo", "pads")
            (t_done, t_hi, t_lo, k_done, k_hi, k_lo, qk_ready, v_done, v_evac, s_done, clipped,
             neg_max_ready, exp_done, pl_copied, vl_ready, pt_done, pt_evac, plt_done, plt_evac, pv_done, pvl_done,
             recip_done, rst_ready, rt_done, even_done, both_done, o_free, recip_split, rst_lo_ready, w2_in, w2_hi, w2_lo,
             pads) = (sem(n, cross) for n in names)
            psT, psK, psV, psS, psO, psM = pb[:, 0, :], (pb[:, 1, :], pb[:, 2, :]), pb[:, 3, :], (pb[:, 4, :], pb[:, 5, :]), pb[:, 6, :], pb[:, 7, :]
            w2_v = w2.rearrange("e (c p) n -> (e c) p n", p=P)

            def over_groups(eng, step):
                for j in range(G):
                    step(0, j, j, False)
                with eng.Fori(1, NG - 1) as i:
                    for j in range(G):
                        step(i, j, i * G + j, False)
                for j in range(G):
                    step(NG - 1, j, (NG - 1) * G + j, True)

            with nc.Block() as block:

                @block.sync
                def _(sp):
                    def load(n, k):
                        src = ctx_v[n] if isinstance(n, int) else ctx_v[bass.ds(n, 1)].rearrange("a p t c -> p (a t) c")
                        sp.dma_start(CX[k][:], src).then_inc(ctx_in[k], 16)

                    for k, w in enumerate((awq, awk, awv, awo)):
                        sp.dma_start(aw_raw[:, k], w.rearrange("(o p) n -> p o n", p=P)).then_inc(raw_in, 16)
                    for k, w in enumerate((w_in, w1)):
                        sp.dma_start(wi_raw[:, :, k, :], w.rearrange("(c p) n -> p c n", p=P)).then_inc(raw_in, 16)
                    sp.dma_start(xwo_raw[:], xwo.rearrange("(c p) n -> p c n", p=P)).then_inc(raw_in, 16)
                    for k, b in enumerate((xbo, abo)):
                        for row in (0, 32):
                            sp.dma_start(brow_raw[row:row + 1, k, :], b.rearrange("(a n) -> a n", a=1)).then_inc(raw_in, 16)
                    with nc.allow_non_contiguous_dma(reason="biases, one element per partition"):
                        for k, b in enumerate((xbv, abq, abk, abv)):
                            sp.dma_start(bcol[:, k, :], b.rearrange("(c p) -> p c", p=P)).then_inc(raw_in, 16)
                    sp.dma_start(gate_b[:], gate_bias.rearrange("(a n) -> a n", a=1).broadcast_to([P, E])).then_inc(raw_in, 16)

                    def step(i, j, n, last):
                        if not last:
                            sp.wait_ge(t_done, n + 1)
                            load(n + 4, j)
                        if j == 0:
                            sp.wait_ge(w2_lo, i)
                            src = w2_v[i] if isinstance(i, int) else w2_v[bass.ds(i, 1)].rearrange("a p n -> p (a n)")
                            sp.dma_start(w2raw[:], src).then_inc(w2_in, 16)

                    over_groups(sp, step)

                @block.gpsimd
                def _(pool):
                    for k in range(2):
                        last_i = nc.gpsimd.memset(KR[k][:, :, :, S:SP_].bitcast(f32), 0.0)
                    last_i.then_inc(pads, 1)

                    def keys_queries(n, k, first):
                        if not first:
                            pool.wait_ge(s_done, (n - 1) * 4)
                        for part, q in enumerate((QTh, QTl)):
                            src = q[:, :, bass.ds(n * T, T)].bitcast(f32).unsqueeze(2).broadcast_to([P, DC, 8, T])
                            msk = head_mask[:].unsqueeze(1).unsqueeze(3).broadcast_to([P, DC, 8, T])
                            nc.gpsimd.tensor_tensor(QB[k][:, part], src, msk, ALU.mult)
                        src = KL[:, bass.ds(n, 1), :, :].bitcast(f32).rearrange("p a c h -> p (a c) h").unsqueeze(3)
                        nc.gpsimd.tensor_copy(KR[k][:, :, :, LAST:S], src).then_inc(qk_ready, 1)

                    keys_queries(0, 0, True)

                    def step(i, j, n, last):
                        if not (last and j == G - 1):
                            keys_queries(n + 1, (j + 1) % 2, False)
                        pool.wait_ge(exp_done, (n + 1) * 4)
                        if j == 0:
                            pool.wait_ge(plt_done, i)
                        apart(pool)
                        nc.gpsimd.tensor_copy(PL[:, :, j], PR[:, :, LAST]).then_inc(pl_copied, 1)
                        if j == G - 1:
                            pool.wait_ge(recip_split, i * 2 + 2)
                            pool.wait_ge(rt_done, i)
                            apart(pool)
                            nc.gpsimd.tensor_tensor(RSTl[:], stacked_id[:].unsqueeze(1).broadcast_to([P, NHG * G, T]),
                                                    recip_lo[:].rearrange("p g b -> p (g b)").unsqueeze(2).broadcast_to([P, NHG * G, T]),
                                                    ALU.mult).then_inc(rst_lo_ready, 1)
                        if j == 1:
                            pool.wait_ge(pvl_done, i)
                            apart(pool)
                            nc.gpsimd.tensor_copy(VLg[:].unsqueeze(1), VL[:, bass.ds(i, 1), :]).then_inc(vl_ready, 1)

                    over_groups(pool, step)

                @block.scalar
                def _(act):
                    def context_hi(n, k, first):
                        act.wait_ge(t_done, n + 1)
                        if not first:
                            act.wait_ge(k_done, (n - 1) * 2)
                        nc.scalar.activation(TR[k][:, 0, :], psT[:, 0:KT * P], ACT.Copy)
                        nc.scalar.activation(TR[k][0:64, 2, :], psT[0:64, KT * P:2 * KT * P], ACT.Copy).then_inc(t_hi, 1)

                    def keys_hi(n, k, first):
                        if not first:
                            act.wait_ge(s_done, (n - 1) * 4)
                        for c in range(DC):
                            act.wait_ge(k_done, n * 2 + c + 1)
                            nc.scalar.activation(KR[k][:, c, 0, 0:LAST], psK[c][:, 0:LAST], ACT.Identity,
                                                 bias=bk[:, c:c + 1]).then_inc(k_hi, 1)

                    def values(n, k, first):
                        act.wait_ge(v_done, n + 1)
                        if not first:
                            act.wait_ge(pv_done, n - 1)
                        nc.scalar.activation(VR[k][:], psV[:, :], ACT.Copy).then_inc(v_evac, 1)

                    context_hi(0, 0, True)
                    context_hi(1, 1, True)
                    keys_hi(0, 0, True)
                    values(0, 0, True)

                    def step(i, j, n, last):
                        act.wait_ge(neg_max_ready, n + 1)
                        act.wait_ge(pt_done, n * 2)
                        act.wait_ge(pl_copied, n)
                        if j == 0:
                            act.wait_ge(recip_done, i)
                        for g in range(NHG):
                            nc.scalar.activation(PR[:, g, :], SC[j % 2][:, g, :], ACT.Exp, bias=neg_max[j % 2][:, g:g + 1],
                                                 accum_out=sums[:, g, j:j + 1]).then_inc(exp_done, 1)
                            if g == 0 and not (last and j == G - 1):
                                keys_hi(n + 1, (j + 1) % 2, False)
                            if g == 1 and not (last and j >= G - 2):
                                context_hi(n + 2, j % 2, False)
                        if not (last and j == G - 1):
                            values(n + 1, (j + 1) % 2, False)
                        if j == 1:
                            act.wait_ge(w2_in, i * 16 + 16)
                            nc.scalar.activation(W2h[:, bass.ds(i, 1), :], w2raw[:].unsqueeze(1), ACT.Copy).then_inc(w2_hi, 1)
                        act.wait_ge(pv_done, n)
                        for kt in range(KT):
                            act.wait_ge(pt_done, n * 2 + kt + 1)
                            nc.scalar.activation(PTs[:, kt, :], psK[kt], ACT.Copy).then_inc(pt_evac, 1)
                        if j == G - 1:
                            act.wait_ge(plt_done, i + 1)
                            act.wait_ge(pvl_done, i)
                            for b in range(G):
                                last_i = nc.scalar.activation(PLT[:, :, b, :], psM[0:G, :].rearrange("p (h q) -> p h q", q=2 * T),
                                                              ACT.Copy, scale=ident[0:G, b:b + 1])
                            last_i.then_inc(plt_evac, 1)

                    over_groups(act, step)

                @block.vector
                def _(dve):
                    def context_lo(n, k):
                        dve.wait_ge(t_hi, n + 1)
                        nc.vector.tensor_tensor(TR[k][:, 1, :], psT[:, 0:KT * P], TR[k][:, 0, :].bitcast(f32), ALU.subtract)
                        nc.vector.tensor_tensor(TR[k][64:P, 2, :], psT[0:64, KT * P:2 * KT * P],
                                                TR[k][0:64, 2, :].bitcast(f32), ALU.subtract).then_inc(t_lo, 1)

                    def keys_lo(n, k):
                        for c in range(DC):
                            dve.wait_ge(k_hi, n * 2 + c + 1)
                            nc.vector.scalar_tensor_tensor(KR[k][:, c, 1, 0:LAST], psK[c][:, 0:LAST], bk[:, c:c + 1],
                                                           KR[k][:, c, 0, 0:LAST].bitcast(f32),
                                                           ALU.add, ALU.subtract).then_inc(k_lo, 1)

                    def clip(n, k, c):
                        if c == 0 and (not isinstance(n, int) or n > 1):
                            dve.wait_ge(exp_done, (n - 1) * 4)
                        for g in (2 * c, 2 * c + 1):
                            dve.wait_ge(s_done, n * 4 + g + 1)
                            nc.vector.tensor_scalar(SC[k][:, g, :], psS[g % 2][:, 0:S], CLAMP, -CLAMP,
                                                    ALU.min, ALU.max).then_inc(clipped, 1)

                    def row_max(n, k):
                        dve.wait_ge(clipped, n * 4 + 4)
                        nc.vector.tensor_reduce(neg_max[k][:], SC[k][:], AX.X, ALU.max, negate=True).then_inc(neg_max_ready, 1)

                    def finish(i):
                        o = psO.rearrange("p (cb e q) -> p cb e q", e=2, q=T)
                        dve.wait_ge(rt_done, i + 1)
                        dve.wait_ge(pv_done, i * G + G)
                        nc.vector.tensor_scalar(even_part[:], o[:, :, 0, :], pair_mask[:, 0:1], None, ALU.mult).then_inc(even_done, 1)
                        dve.wait_ge(even_done, i + 1)
                        nc.vector.scalar_tensor_tensor(even_part[:], o[:, :, 1, :], pair_mask[:, 1:2], even_part[:],
                                                       ALU.mult, ALU.add).then_inc(both_done, 1)
                        dve.wait_ge(both_done, i + 1)
                        nc.vector.tensor_tensor(OT[:, bass.ds(i, 1), :, :].rearrange("p a c t -> p (a c) t"),
                                                even_part[:].rearrange("p (c b) q -> p c (b q)", c=DC),
                                                psM[:, 0:DC * P].rearrange("p (c t) -> p c t", c=DC),
                                                ALU.mult).then_inc(o_free, 1)

                    context_lo(0, 0)
                    context_lo(1, 1)
                    keys_lo(0, 0)
                    for c in range(DC):
                        clip(0, 0, c)
                    row_max(0, 0)

                    def step(i, j, n, last):
                        if not (last and j == G - 1):
                            keys_lo(n + 1, (j + 1) % 2)
                            clip(n + 1, (j + 1) % 2, 0)
                        if not (last and j >= G - 2):
                            context_lo(n + 2, j % 2)
                        if not (last and j == G - 1):
                            clip(n + 1, (j + 1) % 2, 1)
                        if j == G - 1:
                            dve.wait_ge(exp_done, (n + 1) * 4)
                            nc.vector.reciprocal(recip[:], sums[:]).then_inc(recip_done, 1)
                        if not (last and j == G - 1):
                            row_max(n + 1, (j + 1) % 2)
                        if j == 0 and not (isinstance(i, int) and i == 0):
                            finish(i - 1)
                        if j == 1:
                            dve.wait_ge(w2_hi, i + 1)
                            nc.vector.tensor_tensor(W2l[:, bass.ds(i, 1), :], w2raw[:].unsqueeze(1),
                                                    W2h[:, bass.ds(i, 1), :].bitcast(f32), ALU.subtract).then_inc(w2_lo, 1)
                        if j == G - 1:
                            dve.wait_ge(recip_done, i + 1)
                            nc.vector.tensor_copy(recip_hi[:], recip[:]).then_inc(recip_split, 1)
                            dve.wait_ge(recip_split, i * 2 + 1)
                            nc.vector.tensor_tensor(recip_lo[:], recip[:], recip_hi[:].bitcast(f32), ALU.subtract).then_inc(recip_split, 1)
                            dve.wait_ge(rt_done, i)
                            nc.vector.tensor_tensor(RSTh[:], stacked_id[:].unsqueeze(1).broadcast_to([P, NHG * G, T]),
                                                    recip_hi[:].bitcast(f32).rearrange("p g b -> p (g b)").unsqueeze(2).broadcast_to([P, NHG * G, T]),
                                                    ALU.mult).then_inc(rst_ready, 1)

                    over_groups(dve, step)
                    finish(NG - 1)

                @block.tensor
                def _(pe):
                    def transpose_context(n, k, slot, first):
                        pe.wait_ge(ctx_in[slot], (n // 4) * 16 + 16 if isinstance(n, int) else k)
                        if not first:
                            pe.wait_ge(t_lo, n)
                        for t in range(KT):
                            nc.tensor.transpose(psT[:, P * t:P * t + P], CX[slot][:, t, 0:P], ident[:])
                        for t in range(KT):
                            last_i = nc.tensor.transpose(psT[0:64, KT * P + P * t:KT * P + P * t + P], CX[slot][:, t, P:C], ident[:])
                        last_i.then_inc(t_done, 1)

                    def values(n, k, first):
                        pe.wait_ge(t_lo, n + 1)
                        if not first:
                            pe.wait_ge(v_evac, n)
                        passes = ((KVh[:, 1, 0, :], 0), (KVh[:, 1, 0, :], 1), (KVl[:, 1, 0, :], 0),
                                  (KVh[:, 1, 1, :], 2), (KVl[:, 1, 1, :], 2))
                        for kt in range(KT):
                            for m, (w, t) in enumerate(passes):
                                last_i = nc.tensor.matmul(psV[:, D * kt:D * kt + D], TR[k][:, t, P * kt:P * kt + P], w,
                                                          start=m == 0, stop=m == 4)
                        last_i.then_inc(v_done, 1)

                    def keys(n, k, first):
                        if not first:
                            pe.wait_ge(pt_evac, (n - 1) * 2)
                        for c in range(DC):
                            cs = slice(c * P, c * P + P)
                            passes = ((KVh[:, 0, 0, cs], 0), (KVh[:, 0, 0, cs], 1), (KVl[:, 0, 0, cs], 0),
                                      (KVh[:, 0, 1, cs], 2), (KVl[:, 0, 1, cs], 2))
                            for m, (w, t) in enumerate(passes):
                                last_i = nc.tensor.matmul(psK[c][:, 0:LAST], w, TR[k][:, t, :], start=m == 0, stop=m == 4)
                            last_i.then_inc(k_done, 1)

                    def scores(n, k, c, first):
                        pe.wait_ge(k_lo, n * 2 + c + 1)
                        if c == 0:
                            pe.wait_ge(qk_ready, n + 1)
                        for g in (2 * c, 2 * c + 1):
                            if not (first and g < 2):
                                pe.wait_ge(clipped, n * 4 + g - 1)
                            gs = slice(4 * (g % 2), 4 * (g % 2) + 4)
                            q = [QB[k][:, part, c, gs, :].rearrange("p h q -> p (h q)") for part in range(2)]
                            for m, (a, b) in enumerate(((0, 0), (0, 1), (1, 0))):
                                last_i = nc.tensor.matmul(psS[g % 2][:, 0:SP_], q[a], KR[k][:, c, b, :], start=m == 0, stop=m == 2)
                            last_i.then_inc(s_done, 1)

                    def weigh(n, i, j, kt):
                        if kt == 0:
                            if j == 0:
                                pe.wait_ge(o_free, i)
                            pe.wait_ge(v_evac, n + 1)
                        pe.wait_ge(pt_evac, n * 2 + kt + 1)
                        for c in range(DC):
                            o = (c * G + j) * 64
                            for jj in range(4):
                                r = slice(32 * jj, 32 * jj + 32)
                                last_i = nc.tensor.matmul(psO[r, o:o + 64], VR[j % 2][:, kt, c * P + 32 * jj:c * P + 32 * jj + 32],
                                                          PTs[:, kt, (c * 4 + jj) * 64:(c * 4 + jj) * 64 + 64],
                                                          start=(j, kt, c) == (0, 0, 0),
                                                          stop=(j, kt, c) == (G - 1, KT - 1, DC - 1), skip_group_check=True)
                        if kt == KT - 1:
                            last_i.then_inc(pv_done, 1)

                    pe.wait_ge(pads, 1)
                    transpose_context(0, None, 0, True)
                    transpose_context(1, None, 1, False)
                    values(0, 0, True)
                    keys(0, 0, True)
                    for c in range(DC):
                        scores(0, 0, c, True)

                    def finish(i):
                        pe.wait_ge(plt_evac, i + 1)
                        pe.wait_ge(vl_ready, i + 1)
                        apart(pe)
                        for c in range(DC):
                            o = c * G * 64
                            for jj in range(4):
                                r = slice(32 * jj, 32 * jj + 32)
                                last_i = nc.tensor.matmul(psO[r, o:o + G * 64], VLg[:, c * P + 32 * jj:c * P + 32 * jj + 32],
                                                          PLT[:, c * 4 + jj].rearrange("p b q -> p (b q)"),
                                                          start=False, stop=False, skip_group_check=True)
                        last_i.then_inc(pvl_done, 1)
                        pe.wait_ge(rst_ready, i + 1)
                        pe.wait_ge(rst_lo_ready, i + 1)
                        o = psM[:, 0:DC * P].rearrange("p (c n) -> p c n", c=DC)
                        for par in range(2):
                            for m, rst in enumerate((RSTh, RSTl)):
                                rhs = rst[:].rearrange("p (c e b) q -> p e c (b q)", c=DC, e=2)[:, par]
                                last_i = nc.tensor.matmul(o, head_rows[:, par, :], rhs, start=(par, m) == (0, 0), stop=(par, m) == (1, 1))
                        last_i.then_inc(rt_done, 1)

                    def step(i, j, n, last):
                        if not (last and j == G - 1):
                            values(n + 1, (j + 1) % 2, False)
                            keys(n + 1, (j + 1) % 2, False)
                        if not (last and j >= G - 2):
                            transpose_context(n + 2, i * 16 + 16 * ((j + 2) // 4) + 16, (j + 2) % 4, False)
                        if j == 0 and not (isinstance(i, int) and i == 0):
                            finish(i - 1)
                        before = (n - 1, i if j else i - 1, (j - 1) % G)
                        for c in range(DC):
                            if j or not (isinstance(i, int) and i == 0):
                                weigh(*before, c)
                            if not (last and j == G - 1):
                                scores(n + 1, (j + 1) % 2, c, False)
                        pe.wait_ge(exp_done, (n + 1) * 4)
                        for kt in range(KT):
                            for g in range(NHG):
                                last_i = nc.tensor.transpose(psK[kt][:, P * g:P * g + P], PR[:, g, P * kt:P * kt + P], ident[:])
                            last_i.then_inc(pt_done, 1)
                        if j == G - 1:
                            pe.wait_ge(pl_copied, (n + 1))
                            pe.wait_ge(o_free, i)
                            for g in range(NHG):
                                last_i = nc.tensor.transpose(psM[0:G, P * g:P * g + P], PL[:, g, :], ident[:])
                            last_i.then_inc(plt_done, 1)

                    over_groups(pe, step)
                    finish(NG - 1)
                    for kt in range(KT):
                        weigh(B - 1, NG - 1, G - 1, kt)

        XWOh, XWOl = sb("XWOh", [P, DC, D], f32r), sb("XWOl", [P, DC, D], f32r)
        AWh, AWl = sb("AWh", [P, 4, DC, D], f32r), sb("AWl", [P, 4, DC, D], f32r)
        WIh, WIl = sb("WIh", [P, DC, 2, 2 * HID], f32r), sb("WIl", [P, DC, 2, 2 * HID], f32r)
        WSh, WSl = sb("WSh", [P, DC, D], f32r), sb("WSl", [P, DC, D], f32r)
        WGh, WGl = sb("WGh", [P, DC, E], f32r), sb("WGl", [P, DC, E], f32r)
        bias_rows = sb("bias_rows", [64, 2, D], f32r)
        ones_row = sb("ones_row", [64, P], f32r)
        decay = sb("decay", [P, T])
        KTm = sb("KTm", [P, DC, TOK])
        V = OT[:].rearrange("p t c n -> p t (c n)")

        def split_mm(o, pairs, start=True, stop=True):
            n = len(pairs)
            for a, (lhs, rhs) in enumerate(pairs):
                for m, (p, q) in enumerate(((0, 0), (0, 1), (1, 0))):
                    last = nc.tensor.matmul(o, lhs[p], rhs[q], start=start and (a, m) == (0, 0), stop=stop and (a, m) == (n - 1, 2))
            return last

        KB = [sb(f"KB{k}", [P, DC, G, 8, T]) for k in range(2)]
        VM = [sb(f"VM{k}", [P, G, D]) for k in range(2)]
        cols, cols_i = sb("cols", [P, E]), sb("cols_i", [P, E], mybir.dt.int32)

        def block_keys(t, k, c):
            src = KTm[:, c, bass.ds(t * P, P)].rearrange("p (b q) -> p b q", b=G).unsqueeze(2).broadcast_to([P, G, 8, T])
            msk = head_mask[:].unsqueeze(1).unsqueeze(3).broadcast_to([P, G, 8, T])
            return nc.gpsimd.tensor_tensor(KB[k][:, c], src, msk, ALU.mult)

        QS = [sb(f"QS{k}", [P, DC, P]) for k in range(2)]
        logit, shifted, expo, prob = (sb(n, [P, H, T]) for n in ("logit", "shifted", "expo", "prob"))
        probT = sb("probT", [P, H, T])
        nmax, psum_, prec = (sb(n, [P, H]) for n in ("nmax", "psum_", "prec"))
        names = ("staged", "kb_ready", "s_done", "logit_ready", "nmax_ready", "shift_ready", "exp_done", "psum_ready",
                 "prec_ready", "prob_ready", "probT_ready", "pv_done", "even_ready", "both_ready", "o_hi", "o_lo",
                 "j_done", "x2_ready", "st_ready", "mv_ready", "ve_ready", "rs_ready", "xn_ready", "kt_done", "g_hi",
                 "g_lo", "lg_done", "l_done", "lg_read", "gneg_ready", "gexp_done", "th_done", "half_ready",
                 "hid_ready", "grec_ready", "gprob_ready", "top_ready", "idx_ready", "idf_ready", "hot0_ready", "hot_ready",
                 "gw_ready", "m_done", "ht_hi", "ht_lo", "ex_done", "acc_chain", "weighted_ready", "pair_sum",
                 "pairs_ready", "tile_done", "stored")
        F = {n: sem("f_" + n) for n in names}
        psS2, psO2, psJ, psG = pb[:, 0, :], pb[:, 1, :], pb[:, 2, :], pb[:, 3, :]

        def wait(eng, name, value):
            if not isinstance(value, int) or value > 0:
                eng.wait_ge(F[name], value)

        def scores(pe, t, k):
            wait(pe, "kb_ready", t * 2 + 2)
            wait(pe, "staged", t + 1)
            wait(pe, "logit_ready", t)
            for c in range(DC):
                for b in range(G):
                    last = nc.tensor.matmul(psS2[T * b:T * b + T, 256 * c:256 * c + 256], QS[k][:, c, T * b:T * b + T],
                                            KB[k][:, c, b].rearrange("p h q -> p (h q)"), start=c == 0, stop=c == DC - 1,
                                            skip_group_check=True)
            last.then_inc(F["s_done"], 1)

        def stage(act, t, k):
            wait(act, "s_done", t - 1)
            wait(act, "pv_done", t - 1)
            nc.scalar.activation(QS[k][:], QT[:, :, bass.ds(t * P, P)], ACT.Copy)
            for b in range(G):
                r = slice(T * b, T * b + T)
                last = nc.scalar.activation(VM[k][r, b:b + 1, :], V[r, bass.ds(t, 1), :], ACT.Copy)
            last.then_inc(F["staged"], 1)

        def masked(dve, t):
            wait(dve, "s_done", t + 1)
            nc.vector.tensor_tensor(logit[:], psS2.rearrange("p (h k) -> p h k", h=H),
                                    decay[:].unsqueeze(1).broadcast_to([P, H, T]), ALU.add).then_inc(F["logit_ready"], 1)

        def row_max(dve, t):
            wait(dve, "logit_ready", t + 1)
            nc.vector.tensor_reduce(nmax[:], logit[:], AX.X, ALU.max, negate=True).then_inc(F["nmax_ready"], 1)

        def shift(dve, t):
            wait(dve, "nmax_ready", t + 1)
            wait(dve, "exp_done", t)
            nc.vector.tensor_tensor(shifted[:], logit[:], nmax[:].unsqueeze(2).broadcast_to([P, H, T]),
                                    ALU.add).then_inc(F["shift_ready"], 1)

        def exponentials(act, t):
            wait(act, "shift_ready", t + 1)
            wait(act, "prob_ready", t)
            nc.scalar.activation(expo[:], shifted[:], ACT.Exp).then_inc(F["exp_done"], 1)

        def totals(dve, t):
            wait(dve, "exp_done", t + 1)
            nc.vector.tensor_reduce(psum_[:], expo[:], AX.X, ALU.add).then_inc(F["psum_ready"], 1)
            wait(dve, "psum_ready", t + 1)
            nc.vector.reciprocal(prec[:], psum_[:]).then_inc(F["prec_ready"], 1)

        def probabilities(pool, t):
            wait(pool, "prec_ready", t + 1)
            wait(pool, "probT_ready", t)
            nc.gpsimd.tensor_tensor(prob[:], expo[:], prec[:].unsqueeze(2).broadcast_to([P, H, T]),
                                    ALU.mult).then_inc(F["prob_ready"], 1)

        def turn(dve, t):
            wait(dve, "prob_ready", t + 1)
            wait(dve, "pv_done", t)
            nc.vector.transpose(probT[:].rearrange("p h q -> p (h q)"), prob[:].rearrange("p h k -> p (h k)")).then_inc(F["probT_ready"], 1)

        NB = 4
        BW = TOK // NB
        blk = ExitStack()
        with blk:
            oh, ol = sb("oh", [P, DC, BW], f32r, blk), sb("ol", [P, DC, BW], f32r, blk)
            bh, bl = sb("bh", [P, DC, BW], f32r, blk), sb("bl", [P, DC, BW], f32r, blk)
            bq4 = sb("bq4", [P, DC], f32, blk)
            xnb = sb("xnb", [P, 4, D], f32, blk)
            st = sb("st", [P, 4, 6], f32, blk)
            mv = sb("mv", [P, 4, 2], f32, blk)
            ve = sb("ve", [P, 4], f32, blk)
            rs = sb("rs", [P, 4], f32, blk)
            (o_hi, o_lo, y_done, x1_ready, st_ready, mv_ready, ve_ready, rs_ready, xn_done, tr_done, tr_hi, tr_lo,
             p_done, p_evac, bq4_ready, cols_step) = (sem("a_" + n, blk) for n in (
                 "o_hi", "o_lo", "y_done", "x1_ready", "st_ready", "mv_ready", "ve_ready", "rs_ready", "xn_done",
                 "tr_done", "tr_hi", "tr_lo", "p_done", "p_evac", "bq4_ready", "cols_step"))
            ws_raw, wg_raw = sb("ws_raw", [P, DC, D], f32, blk), sb("wg_raw", [P, DC, E], f32, blk)
            brow_hi = sb("brow_hi", [33, 2, D], f32r, blk)
            ii = sb("ii", [P, G, T], mybir.dt.int32, blk)
            dist = [sb(f"dist{k}", [P, G, T], f32, blk) for k in range(4)]
            (ws_in, wg_in, dist_step, awt_done, br_zero, wi_hi, wi_lo, xwo_hi, xwo_lo, br_hi, br_lo, aw_hi,
             aw_lo, s_g_hi) = (sem("w_" + n, blk) for n in (
                 "ws_in", "wg_in", "dist_step", "awt_done", "br_zero", "wi_hi", "wi_lo", "xwo_hi", "xwo_lo",
                 "br_hi", "br_lo", "aw_hi", "aw_lo", "s_g_hi"))
            with nc.Block() as block:

                @block.sync
                def _(sp):
                    sp.dma_start(ws_raw[:], w_out.rearrange("(c p) n -> p c n", p=P)).then_inc(ws_in, 16)
                    sp.dma_start(wg_raw[:], w_gate.rearrange("(c p) n -> p c n", p=P)).then_inc(wg_in, 16)

                def over_blocks(eng, step):
                    step(0, True, False)
                    with eng.Fori(1, NB - 1) as k:
                        step(k, False, False)
                    step(NB - 1, False, True)

                @block.scalar
                def _(act):
                    def split_o(k):
                        act.wait_ge(y_done, k * 4)
                        for c in range(DC):
                            nc.scalar.activation(oh[:, c, :].rearrange("p (t n) -> p t n", n=P), OT[:, bass.ds(k * 4, 4), c, :], ACT.Identity,
                                                 bias=bcol[:, 0, c:c + 1]).then_inc(o_hi, 1)

                    def evacuate(k, outputs=range(6)):
                        act.wait_ge(bq4_ready, 1)
                        act.wait_ge(wi_lo, 2)
                        for m in outputs:
                            act.wait_ge(p_done, k * 6 + m + 1)
                            src = pb[:, 6 + m % 2, :]
                            if m < 2:
                                last = nc.scalar.activation(QT[:, m, bass.ds(k * BW, BW)], src, ACT.Identity,
                                                            bias=bq4[:, m:m + 1], scale=SCALE)
                            elif m < 4:
                                last = nc.scalar.activation(KTm[:, m - 2, bass.ds(k * BW, BW)], src, ACT.Identity,
                                                            bias=bcol[:, 2, m - 2:m - 1])
                            else:
                                last = nc.scalar.activation(V[:, bass.ds(k * 4 + (m - 4) * 2, 2), :],
                                                            src.rearrange("p (t n) -> p t n", n=D), ACT.Copy)
                            last.then_inc(p_evac, 1)

                    act.wait_ge(raw_in, 16 * RAW_LOADS)
                    nc.scalar.activation(XWOh[:], xwo_raw[:], ACT.Copy).then_inc(xwo_hi, 1)
                    split_o(0)
                    act.wait_ge(br_zero, 1)
                    nc.scalar.activation(bias_rows[0:1], brow_raw[0:1], ACT.Copy)
                    nc.scalar.activation(brow_hi[32:33], brow_raw[32:33], ACT.Copy).then_inc(br_hi, 1)
                    for k in range(4):
                        act.wait_ge(awt_done, k + 1)
                        nc.scalar.activation(AWh[:, k], pb[:, 4 + k, :].rearrange("p (c n) -> p c n", c=DC), ACT.Copy).then_inc(aw_hi, 1)
                    for c in range(DC):
                        nc.scalar.activation(WIh[:, c], wi_raw[:, c], ACT.Copy).then_inc(wi_hi, 1)

                    def step(k, first, last):
                        if not last:
                            split_o(k + 1)
                        if first:
                            act.wait_ge(ws_in, 16)
                            nc.scalar.activation(WSh[:], ws_raw[:], ACT.Copy).then_inc(s_g_hi, 1)
                            act.wait_ge(wg_in, 16)
                            nc.scalar.activation(WGh[:], wg_raw[:], ACT.Copy).then_inc(s_g_hi, 1)
                        if not first:
                            evacuate(k - 1)
                        if last:
                            act.wait_ge(p_evac, 6)
                            stage(act, 0, 0)
                        for c in range(DC):
                            act.wait_ge(tr_done, k * 2 + c + 1)
                            if c == 0 and not first:
                                act.wait_ge(p_done, k * 6)
                            nc.scalar.activation(bh[:, c, :], pb[:, 4 + c, :], ACT.Copy).then_inc(tr_hi, 1)

                    over_blocks(act, step)
                    evacuate(NB - 1, range(2))
                    exponentials(act, 0)
                    evacuate(NB - 1, range(2, 6))

                @block.vector
                def _(dve):
                    dve.wait_ge(raw_in, 16 * RAW_LOADS)
                    nc.vector.tensor_scalar(bq4[:], bcol[:, 1, :], SCALE, None, ALU.mult).then_inc(bq4_ready, 1)

                    def split_o(k):
                        for c in range(DC):
                            dve.wait_ge(o_hi, k * 2 + c + 1)
                            nc.vector.scalar_tensor_tensor(ol[:, c, :].rearrange("p (t n) -> p t n", n=P), OT[:, bass.ds(k * 4, 4), c, :],
                                                           bcol[:, 0, c:c + 1], oh[:, c, :].bitcast(f32).rearrange("p (t n) -> p t n", n=P),
                                                           ALU.add, ALU.subtract).then_inc(o_lo, 1)

                    def split_in(k):
                        dve.wait_ge(aw_hi, k + 1)
                        nc.vector.tensor_tensor(AWl[:, k], pb[:, 4 + k, :].rearrange("p (c n) -> p c n", c=DC),
                                                AWh[:, k].bitcast(f32), ALU.subtract).then_inc(aw_lo, 1)

                    nc.vector.memset(ones_row[:].bitcast(f32), 1.0)
                    nc.vector.memset(bias_rows[:].bitcast(f32), 0.0).then_inc(br_zero, 1)
                    dve.wait_ge(xwo_hi, 1)
                    nc.vector.tensor_tensor(XWOl[:], xwo_raw[:], XWOh[:].bitcast(f32), ALU.subtract).then_inc(xwo_lo, 1)
                    split_o(0)
                    dve.wait_ge(br_hi, 1)
                    nc.vector.tensor_tensor(bias_rows[32:33], brow_raw[32:33], brow_hi[32:33].bitcast(f32), ALU.subtract).then_inc(br_lo, 1)
                    split_in(0)
                    split_in(1)

                    def step(k, first, last):
                        for t in range(4):
                            dve.wait_ge(y_done, k * 4 + t + 1)
                            nc.vector.tensor_tensor(X[:, bass.ds(k * 4 + t, 1), :], pb[:, t, 0:D].unsqueeze(1),
                                                    X[:, bass.ds(k * 4 + t, 1), :], ALU.add).then_inc(x1_ready, 1)
                            if t:
                                statistics(k, t - 1)
                        statistics(k, 3)
                        for t in range(4):
                            dve.wait_ge(st_ready, k * 4 + t + 1)
                            apart(dve)
                            nc.vector.bn_aggr(mv[:, t, :], st[:, t, :]).then_inc(mv_ready, 1)
                        if first:
                            split_in(2)
                            split_in(3)
                        dve.wait_ge(rs_ready, k + 1)
                        if not first:
                            dve.wait_ge(tr_done, k * 2)
                        for t in range(4):
                            nc.vector.tensor_scalar(xnb[:, t, :].unsqueeze(1), X[:, bass.ds(k * 4 + t, 1), :], mv[:, t, 0:1],
                                                    rs[:, t:t + 1], ALU.subtract, ALU.mult).then_inc(xn_done, 1)
                        if not last:
                            split_o(k + 1)
                        for c in range(DC):
                            dve.wait_ge(tr_hi, k * 2 + c + 1)
                            nc.vector.tensor_tensor(bl[:, c, :], pb[:, 4 + c, :], bh[:, c, :].bitcast(f32),
                                                    ALU.subtract).then_inc(tr_lo, 1)
                        if first:
                            dve.wait_ge(wi_hi, 2)
                            nc.vector.tensor_tensor(WIl[:, 1], wi_raw[:, 1], WIh[:, 1].bitcast(f32), ALU.subtract).then_inc(wi_lo, 1)
                            dve.wait_ge(s_g_hi, 1)
                            nc.vector.tensor_tensor(WSl[:], ws_raw[:], WSh[:].bitcast(f32), ALU.subtract)
                            dve.wait_ge(s_g_hi, 2)
                            nc.vector.tensor_tensor(WGl[:], wg_raw[:], WGh[:].bitcast(f32), ALU.subtract)
                            dve.wait_ge(dist_step, 5)
                            nc.vector.tensor_reduce(decay[:], dist[3][:].rearrange("p b k -> p k b"), AX.X, ALU.add)

                    def statistics(k, t):
                        dve.wait_ge(x1_ready, k * 4 + t + 1)
                        apart(dve)
                        nc.vector.bn_stats(st[:, t, :], X[:, bass.ds(k * 4 + t, 1), :].rearrange("p a n -> p (a n)")).then_inc(st_ready, 1)

                    over_blocks(dve, step)
                    masked(dve, 0)
                    row_max(dve, 0)
                    shift(dve, 0)
                    totals(dve, 0)
                    turn(dve, 0)

                @block.gpsimd
                def _(pool):
                    def step(k, first, last):
                        if last:
                            for c in range(DC):
                                pool.wait_ge(p_evac, 3 + c)
                                block_keys(0, 0, c).then_inc(F["kb_ready"], 1)
                        pool.wait_ge(mv_ready, k * 4 + 4)
                        if not first:
                            pool.wait_ge(xn_done, k * 4)
                        apart(pool)
                        nc.gpsimd.tensor_scalar(ve[:], mv[:, :, 1], EPS, None, ALU.add).then_inc(ve_ready, 1)
                        pool.wait_ge(ve_ready, k + 1)
                        nc.gpsimd.tensor_tensor(rs[:], ve[:], minus_half[:, 0:4], ALU.pow).then_inc(rs_ready, 1)
                        if first:
                            pool.wait_ge(wi_hi, 1)
                            nc.gpsimd.tensor_tensor(WIl[:, 0], wi_raw[:, 0], WIh[:, 0].bitcast(f32), ALU.subtract).then_inc(wi_lo, 1)

                    nc.gpsimd.iota(ii[:], pattern=[[T, G], [1, T]], base=0, channel_multiplier=-1).then_inc(dist_step, 1)
                    pool.wait_ge(dist_step, 1)
                    nc.gpsimd.tensor_copy(dist[0][:], ii[:]).then_inc(dist_step, 1)
                    pool.wait_ge(dist_step, 2)
                    nc.gpsimd.affine_select(out=dist[1][:], in_=dist[0][:], compare_op=ALU.is_ge, fill=MASKED, base=0,
                                            pattern=[[-T, G], [-1, T]], channel_multiplier=1).then_inc(dist_step, 1)
                    pool.wait_ge(dist_step, 3)
                    nc.gpsimd.affine_select(out=dist[2][:], in_=dist[1][:], compare_op=ALU.is_ge, fill=0.0, base=0,
                                            pattern=[[-T, G], [0, T]], channel_multiplier=1).then_inc(dist_step, 1)
                    pool.wait_ge(dist_step, 4)
                    nc.gpsimd.affine_select(out=dist[3][:], in_=dist[2][:], compare_op=ALU.is_ge, fill=0.0, base=T - 1,
                                            pattern=[[T, G], [0, T]], channel_multiplier=-1).then_inc(dist_step, 1)
                    nc.gpsimd.iota(cols_i[:], pattern=[[1, E]], base=0, channel_multiplier=0).then_inc(cols_step, 1)
                    for k in range(2):
                        nc.gpsimd.memset(VM[k][:], 0.0)
                    pool.wait_ge(cols_step, 1)
                    nc.gpsimd.tensor_copy(cols[:], cols_i[:])
                    over_blocks(pool, step)
                    probabilities(pool, 0)
                    for c in range(DC):
                        block_keys(1, 1, c).then_inc(F["kb_ready"], 1)

                @block.tensor
                def _(pe):
                    pe.wait_ge(raw_in, 16 * RAW_LOADS)
                    for k in range(4):
                        for ic in range(DC):
                            for oc in range(DC):
                                mm = nc.tensor.transpose(pb[:, 4 + k, ic * D + oc * P:ic * D + oc * P + P],
                                                         aw_raw[:, k, oc, ic * P:ic * P + P], ident[:])
                        mm.then_inc(awt_done, 1)

                    def project(k):
                        pe.wait_ge(aw_lo, 4)
                        pe.wait_ge(tr_lo, k * 2 + 2)
                        for m in range(6):
                            if m >= 2:
                                pe.wait_ge(p_evac, k * 6 + m - 1)
                            o = pb[:, 6 + m % 2, :]
                            if m < 4:
                                w, co = m // 2, m % 2
                                last = split_mm(o, [((AWh[:, w, ci, co * P:co * P + P], AWl[:, w, ci, co * P:co * P + P]),
                                                     (bh[:, ci, :], bl[:, ci, :])) for ci in range(DC)])
                            else:
                                for h in range(2):
                                    ts = slice(P * (2 * (m - 4) + h), P * (2 * (m - 4) + h) + P)
                                    last = split_mm(o[:, D * h:D * h + D], [((bh[:, ci, ts], bl[:, ci, ts]),
                                                                            (AWh[:, 2, ci, :], AWl[:, 2, ci, :])) for ci in range(DC)])
                            last.then_inc(p_done, 1)

                    def step(k, first, last):
                        if first:
                            pe.wait_ge(xwo_lo, 1)
                            pe.wait_ge(br_lo, 1)
                        pe.wait_ge(o_lo, k * 2 + 2)
                        for t in range(4):
                            if not first:
                                pe.wait_ge(x1_ready, k * 4 + t - 3)
                            ts = slice(P * t, P * t + P)
                            split_mm(pb[:, t, 0:D], [((oh[:, c, ts], ol[:, c, ts]), (XWOh[:, c, :], XWOl[:, c, :])) for c in range(DC)],
                                     stop=False)
                            nc.tensor.matmul(pb[:, t, 0:D], ones_row[:], bias_rows[:, 0, :], start=False, stop=True).then_inc(y_done, 1)
                        if not first:
                            project(k - 1)
                        for c in range(DC):
                            if first:
                                pe.wait_ge(aw_lo, c + 1)
                            else:
                                pe.wait_ge(tr_lo, k * 2 + c - 1)
                            for t in range(4):
                                pe.wait_ge(xn_done, k * 4 + t + 1)
                                mm = nc.tensor.transpose(pb[:, 4 + c, P * t:P * t + P], xnb[:, t, c * P:c * P + P], ident[:])
                            mm.then_inc(tr_done, 1)

                    over_blocks(pe, step)
                    pe.wait_ge(x1_ready, (NB - 1) * 4 + 1)
                    scores(pe, 0, 0)
                    project(NB - 1)

        fin = ExitStack()
        with fin:
            def sf(name, shape, dt=f32):
                return sb(name, shape, dt, fin)

            even2, both2 = sf("even2", [P, DC * G, T]), sf("both2", [P, DC * G, T])
            o2h, o2l = sf("o2h", [P, DC, P], f32r), sf("o2l", [P, DC, P], f32r)
            st2, mv2, ve2, rs2 = sf("st2", [P, 6]), sf("mv2", [P, 2]), sf("ve2", [P, 1]), sf("rs2", [P, 1])
            xn2 = sf("xn2", [P, D])
            gh, gl = sf("gh", [P, DC, P], f32r), sf("gl", [P, DC, P], f32r)
            th, half, hid = sf("th", [P, 2, HID]), sf("half", [P, 2, HID]), sf("hid", [P, 2, HID])
            HTh = [sf(f"HTh{k}", [P, 2, DC, P], f32r) for k in range(2)]
            HTl = [sf(f"HTl{k}", [P, 2, DC, P], f32r) for k in range(2)]
            lg, gexp, gprob, top8, hot0, hot = (sf(n, [P, E]) for n in ("lg", "gexp", "gprob", "top8", "hot0", "hot"))
            gneg, gsum, grec, idf = sf("gneg", [P, 1]), sf("gsum", [P, 1]), sf("grec", [P, 1]), sf("idf", [P, E])
            idx = sf("idx", [P, E], mybir.dt.uint32)
            gw = [sf(f"gw{k}", [P, E]) for k in range(2)]
            weighted = sf("weighted", [P, 2, 2, D])
            pair2, pair4 = sf("pair2", [P, D]), sf("pair4", [P, D])

            ACC = 5

            def pipeline(eng, step):
                for s in (-1, 0, 1):
                    step(s, s % 2)
                with eng.Fori(1, (NT - 2) // 2) as m:
                    for par in range(2):
                        step(m * 2 + par, par)
                for s in range(NT - 2, NT + 1):
                    step(s, s % 2)

            def attends(s):
                return not isinstance(s, int) or s + 1 < NT

            def starts(s):
                return isinstance(s, int) and s == -1

            def prepares(s):
                return not isinstance(s, int) or s + 2 < NT

            def hides(s):
                return not isinstance(s, int) or 0 <= s < NT

            def expands(s):
                return not isinstance(s, int) or s >= 1

            with nc.Block() as block:

                @block.sync
                def _(sp):
                    out_v = out.rearrange("b t d -> (b t) d").rearrange("(n p) d -> n p d", p=P)

                    with sp.Fori(0, NT) as t:
                        sp.wait_ge(F["tile_done"], t + 1)
                        sp.dma_start(out_v[bass.ds(t, 1)].rearrange("a p n -> p a n"), X[:, bass.ds(t, 1), :]).then_inc(F["stored"], 16)
                    sp.wait_ge(F["stored"], 16 * NT)

                @block.gpsimd
                def _(pool):
                    def add_unit2(t):
                        wait(pool, "weighted_ready", t * 2 + 1)
                        wait(pool, "tile_done", t)
                        nc.gpsimd.tensor_tensor(pair2[:], weighted[:, 0, 0], weighted[:, 0, 1], ALU.add).then_inc(F["pair_sum"], 1)

                    def add_unit4(t):
                        wait(pool, "weighted_ready", t * 2 + 2)
                        nc.gpsimd.tensor_tensor(pair4[:], weighted[:, 1, 0], weighted[:, 1, 1], ALU.add).then_inc(F["pair_sum"], 1)
                        wait(pool, "pair_sum", t * 2 + 2)
                        nc.gpsimd.tensor_tensor(pair4[:], pair2[:], pair4[:], ALU.add).then_inc(F["pairs_ready"], 1)
                        wait(pool, "pairs_ready", t + 1)
                        wait(pool, "acc_chain", t * ACC + ACC)
                        apart(pool)
                        xt = X[:, bass.ds(t, 1), :]
                        nc.gpsimd.tensor_tensor(xt, xt, pair4[:].unsqueeze(1), ALU.add).then_inc(F["tile_done"], 1)

                    def step(s, par):
                        u = s + 1
                        if prepares(s) and not starts(s):
                            wait(pool, "s_done", u)
                            block_keys(s + 2, par, 0).then_inc(F["kb_ready"], 1)
                        if not isinstance(s, int) or s >= 2:
                            add_unit4(s - 2)
                        if attends(s) and not starts(s):
                            probabilities(pool, u)
                        if prepares(s) and not starts(s):
                            block_keys(s + 2, par, 1).then_inc(F["kb_ready"], 1)
                        if expands(s):
                            add_unit2(s - 1)

                        if attends(s):
                            wait(pool, "mv_ready", u + 1)
                            wait(pool, "xn_ready", u)
                            apart(pool)
                            nc.gpsimd.tensor_scalar(ve2[:], mv2[:, 1:2], EPS, None, ALU.add).then_inc(F["ve_ready"], 1)
                            wait(pool, "ve_ready", u + 1)
                            nc.gpsimd.tensor_tensor(rs2[:], ve2[:], minus_half[:, 0:1], ALU.pow).then_inc(F["rs_ready"], 1)

                    pipeline(pool, step)
                    add_unit4(NT - 1)

                @block.scalar
                def _(act):
                    def weigh(t, par, k):
                        m = 2 * k + 2
                        wait(act, "ex_done", t * 5 + m + 1)
                        wait(act, "gw_ready", t + 1)
                        if not isinstance(t, int) or t >= 1:
                            wait(act, "pair_sum", t * 2 - 1 + k)
                        for h in range(2):
                            e = 2 * (m - 1) + h
                            last = nc.scalar.activation(weighted[:, k, h], pb[:, 6 + (m + par) % 2, D * h:D * h + D], ACT.Copy,
                                                        scale=gw[par][:, e:e + 1])
                        last.then_inc(F["weighted_ready"], 1)

                    def step(s, par):
                        u = s + 1
                        if hides(s):
                            wait(act, "kt_done", s + 1)
                            wait(act, "l_done", s * 2)
                            nc.scalar.activation(gh[:], psG[:, 0:D].rearrange("p (c t) -> p c t", c=DC), ACT.Copy).then_inc(F["g_hi"], 1)
                        if attends(s) and not starts(s):
                            exponentials(act, u)
                        if hides(s):
                            wait(act, "l_done", s * 2 + 1)
                            nc.scalar.activation(th[:, 0, :], pb[:, 4, 0:HID], ACT.Tanh, scale=0.5).then_inc(F["th_done"], 1)
                            wait(act, "gneg_ready", s + 1)
                            nc.scalar.activation(gexp[:], lg[:], ACT.Exp, bias=gneg[:], accum_out=gsum[:]).then_inc(F["gexp_done"], 1)
                            wait(act, "l_done", s * 2 + 2)
                            nc.scalar.activation(th[:, 1, :], pb[:, 5, 0:HID], ACT.Tanh, scale=0.5).then_inc(F["th_done"], 1)
                        if prepares(s):
                            stage(act, s + 2, par)
                        if attends(s):
                            wait(act, "both_ready", u + 1)
                            wait(act, "j_done", u)
                            for c in range(DC):
                                last = nc.scalar.activation(o2h[:, c, :].rearrange("p (b q) -> p b q", b=G), both2[:, G * c:G * c + G, :],
                                                            ACT.Identity, bias=bcol[:, 3, c:c + 1])
                            last.then_inc(F["o_hi"], 1)
                        if hides(s):
                            wait(act, "m_done", s + 1)
                            if not isinstance(s, int) or s >= 2:
                                wait(act, "ex_done", (s - 1) * 5)
                            nc.scalar.activation(HTh[par][:], psG.rearrange("p (a c t) -> p a c t", a=2, c=DC), ACT.Copy).then_inc(F["ht_hi"], 1)
                        if expands(s):
                            weigh(s - 1, 1 - par, 0)
                        if expands(s):
                            weigh(s - 1, 1 - par, 1)

                    pipeline(act, step)

                @block.vector
                def _(dve):
                    def accumulate(t, par, m, halves=(0, 1)):
                        xt = X[:, bass.ds(t, 1), :]
                        wait(dve, "ex_done", t * 5 + m + 1)
                        bank = 6 + (m + par) % 2
                        if m == 0:
                            wait(dve, "x2_ready", t + 1)
                            nc.vector.tensor_tensor(xt, pb[:, bank, 0:D].unsqueeze(1), xt, ALU.add).then_inc(F["acc_chain"], 1)
                            return
                        wait(dve, "gw_ready", t + 1)
                        for h in halves:
                            e = 2 * (m - 1) + h
                            wait(dve, "acc_chain", t * ACC + m + h)
                            nc.vector.scalar_tensor_tensor(xt, pb[:, bank, D * h:D * h + D].unsqueeze(1), gw[par][:, e:e + 1], xt,
                                                           ALU.mult, ALU.add).then_inc(F["acc_chain"], 1)

                    def silu_half(s, a):
                        wait(dve, "th_done", s * 2 + a + 1)
                        nc.vector.scalar_tensor_tensor(half[:, a, :], th[:, a, :], 1.0, pb[:, 4 + a, 0:HID], ALU.add, ALU.mult).then_inc(F["half_ready"], 1)

                    def hidden(s, a):
                        wait(dve, "half_ready", s * 2 + a + 1)
                        if a == 0:
                            wait(dve, "m_done", s)
                        nc.vector.scalar_tensor_tensor(hid[:, a, :], half[:, a, :], 0.5, pb[:, 4 + a, HID:2 * HID],
                                                       ALU.mult, ALU.mult).then_inc(F["hid_ready"], 1)

                    def step(s, par):
                        u, po = s + 1, 1 - par
                        if hides(s):
                            wait(dve, "g_hi", s + 1)
                            nc.vector.tensor_tensor(gl[:], psG[:, 0:D].rearrange("p (c t) -> p c t", c=DC), gh[:].bitcast(f32),
                                                    ALU.subtract).then_inc(F["g_lo"], 1)
                        if attends(s) and not starts(s):
                            shift(dve, u)
                        if expands(s):
                            accumulate(s - 1, po, 0)
                        if attends(s) and not starts(s):
                            totals(dve, u)
                        if expands(s):
                            accumulate(s - 1, po, 1)
                        if hides(s):
                            wait(dve, "lg_done", s + 1)
                            wait(dve, "gexp_done", s)
                            nc.vector.tensor_tensor(lg[:], psG[:, 0:E], gate_b[:], ALU.add).then_inc(F["lg_read"], 1)
                            wait(dve, "lg_read", s + 1)
                            nc.vector.tensor_reduce(gneg[:], lg[:], AX.X, ALU.max, negate=True).then_inc(F["gneg_ready"], 1)
                        if attends(s) and not starts(s):
                            turn(dve, u)
                        if hides(s):
                            silu_half(s, 0)
                            wait(dve, "gexp_done", s + 1)
                            nc.vector.reciprocal(grec[:], gsum[:]).then_inc(F["grec_ready"], 1)
                            hidden(s, 0)
                            wait(dve, "grec_ready", s + 1)
                            nc.vector.tensor_scalar(gprob[:], gexp[:], grec[:], None, ALU.mult).then_inc(F["gprob_ready"], 1)
                            silu_half(s, 1)
                            wait(dve, "gprob_ready", s + 1)
                            apart(dve)
                            nc.vector.max(top8[:], gprob[:]).then_inc(F["top_ready"], 1)
                            hidden(s, 1)
                        if attends(s):
                            wait(dve, "pv_done", u + 1)
                            o = psO2.rearrange("p (cb e q) -> p cb e q", e=2, q=T)
                            nc.vector.tensor_scalar(even2[:], o[:, :, 0, :], pair_mask[:, 0:1], None, ALU.mult).then_inc(F["even_ready"], 1)
                        if hides(s):
                            wait(dve, "top_ready", s + 1)
                            apart(dve)
                            nc.vector.max_index(idx[:], top8[:], gprob[:]).then_inc(F["idx_ready"], 1)
                        if attends(s):
                            wait(dve, "even_ready", u + 1)
                            wait(dve, "o_hi", u)
                            nc.vector.scalar_tensor_tensor(both2[:], o[:, :, 1, :], pair_mask[:, 1:2], even2[:], ALU.mult, ALU.add).then_inc(F["both_ready"], 1)
                        if hides(s):
                            wait(dve, "idx_ready", s + 1)
                            nc.vector.tensor_copy(idf[:], idx[:]).then_inc(F["idf_ready"], 1)
                            wait(dve, "idf_ready", s + 1)
                            nc.vector.tensor_scalar(hot0[:], cols[:], idf[:, 0:1], None, ALU.is_equal).then_inc(F["hot0_ready"], 1)
                        if attends(s):
                            wait(dve, "o_hi", u + 1)
                            for c in range(DC):
                                last = nc.vector.scalar_tensor_tensor(o2l[:, c, :].rearrange("p (b q) -> p b q", b=G), both2[:, G * c:G * c + G, :],
                                                                      bcol[:, 3, c:c + 1], o2h[:, c, :].bitcast(f32).rearrange("p (b q) -> p b q", b=G),
                                                                      ALU.add, ALU.subtract)
                            last.then_inc(F["o_lo"], 1)
                        if hides(s):
                            wait(dve, "hot0_ready", s + 1)
                            nc.vector.scalar_tensor_tensor(hot[:], cols[:], idf[:, 1:2], hot0[:], ALU.is_equal, ALU.add).then_inc(F["hot_ready"], 1)
                            wait(dve, "ht_hi", s + 1)
                            nc.vector.tensor_tensor(HTl[par][:].rearrange("p a c t -> p (a c t)"), psG, HTh[par][:].bitcast(f32).rearrange("p a c t -> p (a c t)"),
                                                    ALU.subtract).then_inc(F["ht_lo"], 1)
                            wait(dve, "hot_ready", s + 1)
                            if not isinstance(s, int) or s >= 1:
                                wait(dve, "weighted_ready", (s - 1) * 2)
                            nc.vector.tensor_tensor(gw[par][:], hot[:], gprob[:], ALU.mult).then_inc(F["gw_ready"], 1)
                        if expands(s):
                            accumulate(s - 1, po, 3, (0,))
                        if attends(s):
                            wait(dve, "j_done", u + 1)
                            xu = X[:, bass.ds(u, 1), :]
                            nc.vector.tensor_tensor(xu, psJ[:, 0:D].unsqueeze(1), xu, ALU.add).then_inc(F["x2_ready"], 1)
                            wait(dve, "x2_ready", u + 1)
                            apart(dve)
                            nc.vector.bn_stats(st2[:], xu.rearrange("p a n -> p (a n)")).then_inc(F["st_ready"], 1)
                            wait(dve, "st_ready", u + 1)
                            apart(dve)
                            nc.vector.bn_aggr(mv2[:], st2[:]).then_inc(F["mv_ready"], 1)
                        if prepares(s):
                            masked(dve, s + 2)
                        if expands(s):
                            accumulate(s - 1, po, 3, (1,))
                        if attends(s):
                            wait(dve, "rs_ready", u + 1)
                            wait(dve, "kt_done", u)
                            nc.vector.tensor_scalar(xn2[:].unsqueeze(1), xu, mv2[:, 0:1], rs2[:], ALU.subtract, ALU.mult).then_inc(F["xn_ready"], 1)
                        if prepares(s):
                            row_max(dve, s + 2)

                    pipeline(dve, step)

                @block.tensor
                def _(pe):
                    def experts(t, par, units):
                        wait(pe, "ht_lo", t + 1)
                        for m in units:
                            name, freed = (("acc_chain", t * ACC), ("weighted_ready", t * 2), ("acc_chain", t * ACC + 1),
                                           ("acc_chain", t * ACC + 3), ("weighted_ready", t * 2 + 1))[m]
                            wait(pe, name, freed)
                            bank = 6 + (m + par) % 2
                            if m == 0:
                                last = split_mm(pb[:, bank, 0:D], [((HTh[par][:, 0, c], HTl[par][:, 0, c]), (WSh[:, c], WSl[:, c])) for c in range(DC)])
                            else:
                                last = split_mm(pb[:, bank, :].rearrange("p (e n) -> p e n", e=2),
                                                [((HTh[par][:, 1, c], HTl[par][:, 1, c]),
                                                  (W2h[:, 4 * (m - 1) + c:4 * m:2, :], W2l[:, 4 * (m - 1) + c:4 * m:2, :])) for c in range(DC)])
                            last.then_inc(F["ex_done"], 1)

                    def step(s, par):
                        u, po = s + 1, 1 - par
                        if hides(s):
                            wait(pe, "xn_ready", s + 1)
                            wait(pe, "ht_lo", s)
                            for c in range(DC):
                                last = nc.tensor.transpose(psG[:, P * c:P * c + P], xn2[:, P * c:P * c + P], ident[:])
                            last.then_inc(F["kt_done"], 1)
                        if expands(s):
                            experts(s - 1, po, (0, 1))
                        if hides(s):
                            wait(pe, "g_lo", s + 1)
                            split_mm(psG[:, 0:E], [((gh[:, c], gl[:, c]), (WGh[:, c], WGl[:, c])) for c in range(DC)]).then_inc(F["lg_done"], 1)
                            wait(pe, "hid_ready", s * 2)
                            for a in range(2):
                                split_mm(pb[:, 4 + a, :], [((gh[:, c], gl[:, c]), (WIh[:, c, a, :], WIl[:, c, a, :])) for c in range(DC)]).then_inc(F["l_done"], 1)
                        if attends(s):
                            wait(pe, "probT_ready", u + 1)
                            wait(pe, "both_ready", u)
                            for b in range(G):
                                for c in range(DC):
                                    o = (c * G + b) * 64
                                    for jj in range(4):
                                        h0 = c * 8 + 2 * jj
                                        last = nc.tensor.matmul(psO2[32 * jj:32 * jj + 32, o:o + 64], VM[po][:, b, c * P + 32 * jj:c * P + 32 * jj + 32],
                                                                probT[:, h0:h0 + 2, :].rearrange("p h q -> p (h q)"), start=(b, c) == (0, 0),
                                                                stop=(b, c) == (G - 1, DC - 1), skip_group_check=True)
                            last.then_inc(F["pv_done"], 1)
                        if expands(s):
                            experts(s - 1, po, (2,))
                        if hides(s):
                            wait(pe, "hid_ready", s * 2 + 2)
                            wait(pe, "lg_read", s + 1)
                            for a in range(2):
                                for c in range(DC):
                                    o = (a * DC + c) * P
                                    last = nc.tensor.transpose(psG[:, o:o + P], hid[:, a, P * c:P * c + P], ident[:])
                            last.then_inc(F["m_done"], 1)
                        if expands(s):
                            experts(s - 1, po, (3,))
                        if attends(s):
                            wait(pe, "o_lo", u + 1)
                            wait(pe, "x2_ready", u)
                            split_mm(psJ[:, 0:D], [((o2h[:, c], o2l[:, c]), (AWh[:, 3, c, :], AWl[:, 3, c, :])) for c in range(DC)], stop=False)
                            nc.tensor.matmul(psJ[:, 0:D], ones_row[:], bias_rows[:, 1, :], start=False, stop=True).then_inc(F["j_done"], 1)
                        if prepares(s):
                            scores(pe, s + 2, par)
                        if expands(s):
                            experts(s - 1, po, (4,))

                    pipeline(pe, step)


_INS = ['x', 'ctx_768', 'L0_xattn_Wq', 'L0_xattn_bq', 'L0_xattn_Wk', 'L0_xattn_bk', 'L0_xattn_Wv', 'L0_xattn_bv',
        'L0_xattn_Wo', 'L0_xattn_bo', 'L0_attn_Wq', 'L0_attn_bq', 'L0_attn_Wk', 'L0_attn_bk', 'L0_attn_Wv',
        'L0_attn_bv', 'L0_attn_Wo', 'L0_attn_bo', 'L0_ffn_w_shared_in', 'L0_ffn_w_shared_out', 'L0_ffn_w1_shared',
        'L0_ffn_w2', 'L0_ffn_w_gate', 'L0_ffn_gate_bias']
_OUTS = [((64, 32, 256), 'float32')]


def kernel(**inputs):
    import numpy as _np
    import concourse.bacc as _bacc
    from concourse import mybir as _mybir
    from concourse.bass_utils import run_bass_kernel_spmd as _run

    nc = _bacc.Bacc("TRN2", target_bir_lowering=False, num_devices=1)
    arrays, args = {}, []
    for name in _INS:
        a = _np.ascontiguousarray(inputs[name])
        arrays[f"in_{name}_dram"] = a
        args.append(nc.dram_tensor(f"in_{name}_dram", a.shape, _mybir.dt.from_np(a.dtype), kind="ExternalInput").ap())
    for i, (shape, dtype) in enumerate(_OUTS):
        dt = _mybir.dt.from_np(_np.dtype(dtype))
        args.append(nc.dram_tensor(f"out_{i}_dram", shape, dt, kind="ExternalOutput").ap())
    perceiver_kernel(nc, *args)
    r = _run(nc, [arrays], core_ids=[0])
    got = tuple(r.results[0][f"out_{i}_dram"] for i in range(len(_OUTS)))
    return got[0]
```
